# Optimizing a Trainium2 kernel written in Bass

```python
import numpy as np
import jax
import jax.numpy as jnp

def _softmax(x, axis=-1):
    return jax.nn.softmax(x, axis=axis)

def _gelu(x):
    return jax.nn.gelu(x, approximate=True)

def _silu(x):
    return jax.nn.silu(x)

def _sigmoid(x):
    return jax.nn.sigmoid(x)

def _layernorm(x, axis=-1, eps=1e-05):
    m = jnp.mean(x, axis=axis, keepdims=True)
    v = jnp.var(x, axis=axis, keepdims=True)
    return (x - m) / jnp.sqrt(v + eps)

def _scatter_add(tgt, idx, src, axis=0):
    return tgt.at[idx].add(src)

def _segment_sum(src, seg, n):
    return jax.ops.segment_sum(src, seg, n)
kernel_name = 'mk_gnn_resnorm_d2_gnn_r64_1a8d89'

def setup_inputs(seed: int=0):
    np.random.seed(seed)
    _w = jnp.asarray

    def _rec_inputs():
        import jax
        import jax.numpy as jnp
        _gk = jax.random.key(seed)
        x = -0.000202 + 1 * jax.random.normal(jax.random.fold_in(_gk, 1), (50000, 128), jnp.float32)
        src = jax.random.randint(jax.random.fold_in(_gk, 2), (25000,), 0, 50000, jnp.int32)
        dst = jnp.minimum((50000 * jax.random.uniform(jax.random.fold_in(_gk, 3), (25000,)) ** 2.0).astype(jnp.int32), 49999)
        _o = jnp.argsort(dst, stable=True)
        src = src[_o]
        dst = dst[_o]
        edge_attr_128 = -5.16925e-05 + 1.00005 * jax.random.normal(jax.random.fold_in(_gk, 11), (25000, 128), jnp.float32)
        return (x, src, dst, edge_attr_128)
    x, src, dst, edge_attr_128 = _rec_inputs()

    def _L0_gnn_setup():
        import jax, jax.numpy as jnp
        import numpy as np
        N_NODES = 50000
        N_EDGES = 12500
        F_X = 128
        F_E = 128
        HID = 256
        F_OUT = 128
        key = jax.random.key(seed)
        k1, k2, k3, k4, k5 = jax.random.split(key, 5)
        x = jax.random.normal(k1, (N_NODES, F_X), dtype=jnp.float32)
        edge_index = jax.random.randint(k2, (2, N_EDGES), 0, N_NODES, dtype=jnp.int64)
        edge_attr = jax.random.normal(k3, (N_EDGES, F_E), dtype=jnp.float32)
        din = F_X + F_E
        W1 = jax.random.normal(k4, (din, HID), dtype=jnp.float32) * (1.0 / np.sqrt(din))
        b1 = jnp.zeros((HID,), dtype=jnp.float32)
        W2 = jax.random.normal(k5, (HID, F_OUT), dtype=jnp.float32) * (1.0 / np.sqrt(HID))
        b2 = jnp.zeros((F_OUT,), dtype=jnp.float32)
        return {'x': x, 'edge_index': edge_index, 'edge_attr': edge_attr, 'W1': W1, 'b1': b1, 'W2': W2, 'b2': b2}
    _L0_gnn_all = _L0_gnn_setup()
    _L0_gnn_in = {k: v for k, v in _L0_gnn_all.items() if k in ('W1', 'b1', 'W2', 'b2')}
    del _L0_gnn_all

    def _L1_gnn_setup():
        import jax, jax.numpy as jnp
        import numpy as np
        N_NODES = 50000
        EMBED_DIM = 128
        NUM_HEADS = 8
        N_EDGES = 12500
        key = jax.random.key(seed)
        k1, k2, k3, k4 = jax.random.split(key, 4)
        node_states = jax.random.normal(k1, (N_NODES, EMBED_DIM), dtype=jnp.float32)
        edges = jax.random.randint(k2, (2, N_EDGES), 0, N_NODES, dtype=jnp.int64)
        fan_in, fan_out = (EMBED_DIM, 3 * EMBED_DIM)
        g = 1.0 / np.sqrt(2.0) * np.sqrt(6.0 / (fan_in + fan_out))
        qkv_w = jax.random.uniform(k3, (3 * EMBED_DIM, EMBED_DIM), dtype=jnp.float32, minval=-g, maxval=g)
        qkv_b = jnp.zeros((3 * EMBED_DIM,), dtype=jnp.float32)
        g2 = np.sqrt(6.0 / (2 * EMBED_DIM))
        out_w = jax.random.uniform(k4, (EMBED_DIM, EMBED_DIM), dtype=jnp.float32, minval=-g2, maxval=g2)
        out_b = jnp.zeros((EMBED_DIM,), dtype=jnp.float32)
        return {'node_states': node_states, 'edges': edges, 'qkv_w': qkv_w, 'qkv_b': qkv_b, 'out_w': out_w, 'out_b': out_b}
    _L1_gnn_all = _L1_gnn_setup()
    _L1_gnn_in = {k: v for k, v in _L1_gnn_all.items() if k in ('qkv_w', 'qkv_b', 'out_w', 'out_b')}
    del _L1_gnn_all
    return {'x': x, 'src': src, 'dst': dst, 'edge_attr_128': edge_attr_128, 'L0_gnn_W1': _L0_gnn_in['W1'], 'L0_gnn_b1': _L0_gnn_in['b1'], 'L0_gnn_W2': _L0_gnn_in['W2'], 'L0_gnn_b2': _L0_gnn_in['b2'], 'L1_gnn_qkv_w': _L1_gnn_in['qkv_w'], 'L1_gnn_qkv_b': _L1_gnn_in['qkv_b'], 'L1_gnn_out_w': _L1_gnn_in['out_w'], 'L1_gnn_out_b': _L1_gnn_in['out_b']}

def reference(x, src, dst, edge_attr_128, L0_gnn_W1, L0_gnn_b1, L0_gnn_W2, L0_gnn_b2, L1_gnn_qkv_w, L1_gnn_qkv_b, L1_gnn_out_w, L1_gnn_out_b):
    import jax
    import jax.numpy as jnp

    def _L0_gnn_ref(x, edge_index, edge_attr, W1, b1, W2, b2):
        import jax, jax.numpy as jnp
        import numpy as np
        N_NODES = 50000
        N_EDGES = 12500
        F_X = 128
        F_E = 128
        HID = 256
        F_OUT = 128
        num_nodes = x.shape[0]
        dst = edge_index[1]
        sums = jax.ops.segment_sum(edge_attr, dst, num_segments=num_nodes)
        ones = jnp.ones((edge_attr.shape[0],), dtype=edge_attr.dtype)
        counts = jax.ops.segment_sum(ones, dst, num_segments=num_nodes)
        agg = sums / jnp.maximum(counts, 1.0)[:, None]
        node_inputs = jnp.concatenate([x, agg], axis=-1)
        h = jax.nn.relu(node_inputs @ W1 + b1)
        return h @ W2 + b2

    def _L1_gnn_ref(node_states, edges, qkv_w, qkv_b, out_w, out_b):
        import jax, jax.numpy as jnp
        import numpy as np
        N_NODES = 50000
        EMBED_DIM = 128
        NUM_HEADS = 8
        N_EDGES = 12500
        N, E = node_states.shape
        H = NUM_HEADS
        hd = E // H
        src = edges[0]
        tgt = edges[1]
        qkv = node_states @ qkv_w.T + qkv_b
        q, k, v = jnp.split(qkv, 3, axis=1)
        qe = q[tgt]
        ke = k[src]
        ve = v[src]
        scores = (qe * ke).reshape(-1, H, hd).sum(-1) * float(hd) ** (-0.5)
        smax = jax.ops.segment_max(scores, tgt, num_segments=N)
        ex = jnp.exp(scores - smax[tgt])
        denom = jax.ops.segment_sum(ex, tgt, num_segments=N)
        w = ex / denom[tgt]
        msg = (ve.reshape(-1, H, hd) * w[:, :, None]).reshape(-1, E)
        attn_out = jax.ops.segment_sum(msg, tgt, num_segments=N)
        return attn_out @ out_w.T + out_b
    edge_index = jnp.stack([src, dst])
    x = _layernorm(x + _L0_gnn_ref(x, edge_index, edge_attr_128, L0_gnn_W1, L0_gnn_b1, L0_gnn_W2, L0_gnn_b2), axis=-1)
    x = _layernorm(x + _L1_gnn_ref(x, edge_index, L1_gnn_qkv_w, L1_gnn_qkv_b, L1_gnn_out_w, L1_gnn_out_b), axis=-1)
    return x

_drawn_inputs = setup_inputs


def setup_inputs(seed=0):
    import zlib

    import numpy as np

    out = dict(_drawn_inputs(seed))
    spreads = {'L0_gnn_b1': (0.0, 0.1),
     'L0_gnn_b2': (0.0, 0.1),
     'L1_gnn_qkv_b': (0.0, 0.1),
     'L1_gnn_out_b': (0.0, 0.1)}
    factors = {}
    for name, (base, spread) in spreads.items():
        noise = np.random.default_rng([zlib.crc32(name.encode()), seed]).standard_normal(out[name].shape)
        drawn = base * np.exp(spread * noise) if base else spread * noise
        out[name] = jnp.asarray(drawn.astype(out[name].dtype))
    for name, factor in factors.items():
        out[name] = (out[name] * factor).astype(out[name].dtype)
    return out
```

```python
from contextlib import ExitStack

import concourse.bass as bass
from concourse import mybir

F32 = mybir.dt.float32
BF16 = mybir.dt.bfloat16
I32 = mybir.dt.int32
ALU = mybir.AluOpType
ACT = mybir.ActivationFunctionType

P = 128
NODES = 50000
EDGES = 25000
TILES = 4
GROUP = TILES * P
NG = -(-NODES // GROUP)
EG = -(-EDGES // GROUP)
EPAD = EG * GROUP
ET = EPAD // P
EROW = EPAD // P
HID = 256
HEADS = 8
HD = P // HEADS
EPS = 1e-5
FAR = 1.0e30
PAD_NODE = NODES
SKIP = 65536.0
ZROWS = 24
ZSTEP = P * ZROWS


def build(nc, x, attr, dst_tile, next_tile, src_tile, dst_row, prev_row, w1, b1, w2, b2, qkv_wT, qkv_b, out_wT,
          out_b, ident_c, head_sum_c, head_pick_c, out):
    agg_d = nc.dram_tensor("agg_scratch", (NODES, P), F32).ap()
    x1_d = nc.dram_tensor("x1_scratch", (NODES, P), F32).ap()
    same_d = nc.dram_tensor("same_scratch", (EPAD,), BF16).ap()
    reset_d = nc.dram_tensor("reset_scratch", (EPAD,), BF16).ap()
    rcount_d = nc.dram_tensor("rcount_scratch", (EPAD,), F32).ap()
    bias_d = nc.dram_tensor("bias_scratch", (6, P), BF16).ap()

    ctx = ExitStack()
    with ctx:
        def sb(name, shape, dt=F32):
            return ctx.enter_context(nc.sbuf_tensor(name, shape, dt))

        def sem(name):
            return ctx.enter_context(nc.semaphore(name))

        ident = sb("ident", [P, P])
        head_sum = sb("head_sum", [P, P])
        head_pick = sb("head_pick", [P, HEADS])
        w1_sb = sb("w1_sb", [P, 2, HID])
        w2_sb = sb("w2_sb", [P, 2, P])
        qkvw_sb = sb("qkvw_sb", [P, 3 * P])
        outw_sb = sb("outw_sb", [P, P])
        b1_sb = sb("b1_sb", [P, 2])
        qkvb_sb = sb("qkvb_sb", [P, 3])
        outb_bc = sb("outb_bc", [P, P])
        bias_row = sb("bias_row", [1, 2, P])
        bias_left = sb("bias_left", [1, 2, 2, P])
        bias_part = sb("bias_part", [1, 3, 2, P], BF16)
        bias3 = sb("bias3", [3, 2, P], BF16)
        ones3 = sb("ones3", [3, P], BF16)
        one1 = sb("one1", [1, 1])
        eps = sb("eps", [P, 1])
        zeros = sb("zeros", [P, 8 * P])

        dst_i = sb("dst_i", [P, ET], I32)
        next_i = sb("next_i", [P, ET], I32)
        src_i = sb("src_i", [P, ET], I32)
        dst_f = sb("dst_f", [P, ET])
        next_f = sb("next_f", [P, ET])
        inner_f = sb("inner_f", [P, ET])
        scatter_f = sb("scatter_f", [P, ET])
        gather_f = sb("gather_f", [P, ET])
        scatter_i = sb("scatter_i", [P, ET], I32)
        gather_i = sb("gather_i", [P, ET], I32)
        rcount_t = sb("rcount_t", [P, ET])
        cur_r = sb("cur_r", [P, EROW], I32)
        prev_r = sb("prev_r", [P, EROW], I32)
        cur_rf = sb("cur_rf", [P, EROW])
        prev_rf = sb("prev_rf", [P, EROW])
        same_r = sb("same_r", [P, EROW])
        same_bf = sb("same_bf", [P, EROW], BF16)
        reset_bf = sb("reset_bf", [P, EROW], BF16)
        edge_no_i = sb("edge_no_i", [P, EROW], I32)
        edge_no = sb("edge_no", [P, EROW])
        first_r = sb("first_r", [P, EROW])
        start_r = sb("start_r", [P, EROW])
        start_row = sb("start_row", [1, P + 1])
        start_in = sb("start_in", [P, 1])
        count_r = sb("count_r", [P, EROW])
        rcount_r = sb("rcount_r", [P, EROW])
        rcount_l = sb("rcount_l", [ET // 2, 2, P])

        attr_sb = sb("attr_sb", [P, 4, TILES, P])
        attr_tail = sb("attr_tail", [P, TILES, P])
        same_sb = sb("same_sb", [P, 4, GROUP], BF16)
        sumT = sb("sumT", [P, 4, GROUP])
        mean = sb("mean", [P, 4, TILES, P])
        scat_idx = sb("scat_idx", [P, 4, TILES], I32)

        xn = sb("xn", [P, 4, TILES, P])
        an = sb("an", [P, 4, TILES, P])
        xT = sb("xT", [P, 2, GROUP])
        aT = sb("aT", [P, 2, GROUP])
        hT = sb("hT", [P, 2, 2, GROUP])
        z1 = sb("z1", [P, 4, TILES, P])
        x1 = sb("x1", [P, 4, TILES, P])
        z2 = sb("z2", [P, 4, TILES, P])
        o2 = sb("o2", [P, 4, TILES, P])
        st1 = sb("st1", [P, 2, TILES, 6])
        mv1 = sb("mv1", [P, 4, TILES, 2])
        sd1 = sb("sd1", [P, 4, TILES])
        rs1 = sb("rs1", [P, 4, TILES])
        st2 = sb("st2", [P, 2, TILES, 6])
        mv2 = sb("mv2", [P, 4, TILES, 2])
        sd2 = sb("sd2", [P, 4, TILES])
        rs2 = sb("rs2", [P, 4, TILES])
        nb2 = sb("nb2", [P, 4, TILES])

        src_idx = sb("src_idx", [P, 4, TILES], I32)
        dst_idx = sb("dst_idx", [P, 4, TILES], I32)
        out_idx = sb("out_idx", [P, 4, TILES], I32)
        xs = sb("xs", [P, 2, TILES, P])
        xd = sb("xd", [P, 4, TILES, P])
        reset_sb = sb("reset_sb", [P, 4, GROUP], BF16)
        xsT = sb("xsT", [P, 2, GROUP])
        xdT = sb("xdT", [P, 2, GROUP])
        qT = sb("qT", [P, GROUP])
        qk = sb("qk", [P, GROUP])
        mx = sb("mx", [P, 4, GROUP + 1])
        keep = sb("keep", [P, GROUP])
        drop = sb("drop", [P, GROUP])
        rise = sb("rise", [P, GROUP])
        decay = sb("decay", [P, GROUP])
        prob = sb("prob", [P, GROUP])
        pv = sb("pv", [P, GROUP])
        den = sb("den", [P, 2, GROUP])
        acc = sb("acc", [P, 2, GROUP])
        rden = sb("rden", [P, TILES, HEADS])
        attn = sb("attn", [P, TILES, P])
        attnT = sb("attnT", [P, GROUP])
        z3 = sb("z3", [P, 2, TILES, P])
        st3 = sb("st3", [P, TILES, 6])
        mv3 = sb("mv3", [P, 2, TILES, 2])
        ln3 = sb("ln3", [P, TILES])
        rs3 = sb("rs3", [P, 2, TILES])
        nb3 = sb("nb3", [P, 2, TILES])
        o3 = sb("o3", [P, 4, TILES, P])

        banks = [ctx.enter_context(nc.psum_tensor(f"bank{i}", [P, GROUP], F32)) for i in range(8)]

        names = """weights_in rows_in tiles_in attr_tail_in zeroed bias_out bias_in masks_out rcount_out rcount_in
            consts_set zeros_set iota_done gate_sp gate_dve setup_v setup_t setup_c gate
            a_T a_scan a_back a_mean a_idx
            n_T n_evac n_h n_relu n_y n_z n_stats n_aggr n_sd n_rs n_x1 n_z2 n_stats2 n_aggr2 n_sd2 n_rs2 n_nb2 n_out
            e_idx e_idx2 e_T e_evac e_q e_k e_v e_qT e_qk e_s e_mx e_keep e_drop e_rise e_decay e_prob e_pv e_den e_acc
            e_back e_rden e_attn e_attnT e_attnTs e_o e_z e_stats e_aggr e_ln e_rs e_nb e_out e_carry""".split()
        s = {n: sem(n) for n in names}
        attr_in = [sem(f"attr_in{k}") for k in range(4)]
        same_in = [sem(f"same_in{k}") for k in range(4)]
        mean_out = [sem(f"mean_out{k}") for k in range(4)]
        node_in = [sem(f"node_in{k}") for k in range(4)]
        x1_out = [sem(f"x1_out{k}") for k in range(4)]
        o2_out = [sem(f"o2_out{k}") for k in range(4)]
        reset_in = [sem(f"reset_in{k}") for k in range(4)]
        gathered = [sem(f"gathered{k}") for k in range(4)]
        o3_out = [sem(f"o3_out{k}") for k in range(4)]

        def steps(eng, total, lag, body):
            first = -(-(4 + lag) // 4) * 4
            last = (total - 1) // 4 * 4
            for g in range(first):
                body(g, g % 4)
            with eng.Fori(first // 4, last // 4) as i:
                for k in range(4):
                    body(i * 4 + k, k)
            for g in range(last, total + lag):
                body(g, g % 4)

        def inside(g, total):
            return not isinstance(g, int) or 0 <= g < total

        def wait(eng, semaphore, value):
            if not isinstance(value, int) or value > 0:
                eng.wait_ge(semaphore, value)

        def uses(g, k):
            return (g - k) // 4 + 1 if isinstance(g, int) else None

        def slot_count(g, k, per, back=0):
            if isinstance(g, int):
                return ((g - k) // 4 + 1 - back) * per
            return (g - k) * (per // 4) + (1 - back) * per

        def node_base(g):
            return min(g * GROUP, NODES - GROUP) if isinstance(g, int) else g * GROUP

        def node_rows(t, g):
            return t[bass.ds(node_base(g), GROUP), :].rearrange("(p j) f -> p j f", j=TILES)

        def stand(eng, gate):
            eng.sem_inc(s[gate], 1)

        block = ctx.enter_context(nc.Block())

        @block.sync
        def _(sp):
            for t, src in ((cur_r, dst_row), (prev_r, prev_row)):
                sp.dma_start(t[:, :], src).then_inc(s["rows_in"], 16)
            for t, src in ((dst_i, dst_tile), (next_i, next_tile), (src_i, src_tile)):
                sp.dma_start(t[:, :], src).then_inc(s["tiles_in"], 16)
            for t, src in (
                (ident[:, :], ident_c), (head_sum[:, :], head_sum_c), (head_pick[:, :], head_pick_c),
                (w1_sb[:, :, :], w1.rearrange("(c p) h -> p c h", p=P)),
                (w2_sb[:, :, :], w2.rearrange("(c p) h -> p c h", p=P)),
                (qkvw_sb[:, :], qkv_wT), (outw_sb[:, :], out_wT), (b1_sb[:, :], b1), (qkvb_sb[:, :], qkv_b),
                (outb_bc[:, :], out_b.to_broadcast((P, P))),
                (bias_row[:, 0, :], b2), (bias_row[:, 1, :], out_b),
            ):
                sp.dma_start(t, src).then_inc(s["weights_in"], 16)
            sp.wait_ge(s["zeros_set"], 2)
            full = (EDGES - (EG - 1) * GROUP) // P
            rest = EDGES - (EG - 1) * GROUP - full * P
            tail = attr[(EG - 1) * GROUP:, :]
            sp.dma_start(attr_tail[:, 0:full, :], tail[0:full * P, :].rearrange("(j p) f -> p j f", p=P))\
                .then_inc(s["attr_tail_in"], 16)
            sp.dma_start(attr_tail[0:rest, full, :], tail[full * P:full * P + rest, :])\
                .then_inc(s["attr_tail_in"], 16)
            sp.wait_ge(s["rcount_out"], 16)
            sp.dma_start(rcount_l[:, :, :], rcount_d.rearrange("(b t p) -> t b p", b=2, p=P))\
                .then_inc(s["rcount_in"], 16)
            sp.wait_ge(s["bias_out"], 16)
            sp.dma_start(bias3[:, :, :], bias_d.rearrange("(k b) f -> k b f", b=2)).then_inc(s["bias_in"], 16)
            sp.wait_ge(s["masks_out"], 32)

            def edge_load(g, k):
                if not isinstance(g, int) or g < EG - 1:
                    wait(sp, s["a_T"], g - 3)
                    stand(sp, "gate_sp")
                    sp.dma_start(attr_sb[:, k, :, :],
                                 attr[bass.ds(g * GROUP, GROUP), :].rearrange("(j p) f -> p j f", p=P))\
                        .then_inc(attr_in[k], 16)
                if inside(g, EG):
                    wait(sp, s["a_scan"], g - 3)
                    stand(sp, "gate_sp")
                    sp.dma_start(same_sb[:, k, :],
                                 same_d[bass.ds(g * GROUP, GROUP)].unsqueeze(0).to_broadcast((P, GROUP)))\
                        .then_inc(same_in[k], 16)

            steps(sp, EG, 0, edge_load)

            for k in range(4):
                sp.wait_ge(mean_out[k], slot_count((EG - 1 - k) // 4 * 4 + k, k, 64))

            def node_io(g, k):
                if inside(g, NG):
                    wait(sp, s["n_T"], g - 3)
                    wait(sp, s["n_z"], g - 3)
                    stand(sp, "gate_sp")
                    sp.dma_start(xn[:, k, :, :], node_rows(x, g)).then_inc(node_in[k], 16)
                    sp.dma_start(an[:, k, :, :], node_rows(agg_d, g)).then_inc(node_in[k], 16)
                h = g - 4
                if inside(h, NG):
                    sp.wait_ge(s["n_x1"], h + 1)
                    if isinstance(h, int) and h == NG - 1:
                        sp.wait_ge(x1_out[(h - 1) % 4], slot_count(h - 1, (h - 1) % 4, 16))
                    stand(sp, "gate_sp")
                    sp.dma_start(node_rows(x1_d, h), x1[:, k, :, :]).then_inc(x1_out[k], 16)
                h = g - 7
                if inside(h, NG):
                    sp.wait_ge(s["n_out"], h + 1)
                    if isinstance(h, int) and h == NG - 1:
                        sp.wait_ge(o2_out[(h - 1) % 4], slot_count(h - 1, (h - 1) % 4, 16))
                    stand(sp, "gate_sp")
                    sp.dma_start(node_rows(out, h), o2[:, (k - 7) % 4, :, :]).then_inc(o2_out[(k - 7) % 4], 16)

            steps(sp, NG, 7, node_io)

            def reset_load(g, k):
                if inside(g, EG):
                    wait(sp, s["e_keep"], g - 3)
                    stand(sp, "gate_sp")
                    sp.dma_start(reset_sb[:, k, :],
                                 reset_d[bass.ds(g * GROUP, GROUP)].unsqueeze(0).to_broadcast((P, GROUP)))\
                        .then_inc(reset_in[k], 16)

            steps(sp, EG, 0, reset_load)

        @block.gpsimd
        def _(pool):
            nc.gpsimd.iota(edge_no_i[:, :], pattern=[[1, EROW]], base=0, channel_multiplier=EROW)\
                .then_inc(s["iota_done"], 1)

            def scatter(target, index, rows, done, k):
                for j in range(TILES):
                    pool.indirect_dma_start(
                        out=target, out_offset=bass.IndirectOffsetOnAxis(ap=index[:, k, j:j + 1], axis=0),
                        in_=rows[:, k, j, :], in_offset=None, bounds_check=NODES - 1, oob_is_err=False,
                    ).then_inc(done, 16)

            def gather(source, index, rows, k, kr, done):
                for j in range(TILES):
                    pool.indirect_dma_start(
                        out=rows[:, kr, j, :], out_offset=None, in_=source,
                        in_offset=bass.IndirectOffsetOnAxis(ap=index[:, k, j:j + 1], axis=0),
                        bounds_check=NODES - 1, oob_is_err=False,
                    ).then_inc(done, 16)

            pool.wait_ge(s["setup_v"], 20)
            pool.wait_ge(s["zeroed"], 16 * (NODES // ZSTEP + 1))

            def scatter_means(g, k):
                if inside(g, EG):
                    wait(pool, mean_out[k], slot_count(g, k, 64, 1))
                    stand(pool, "gate")
                    nc.gpsimd.tensor_copy(scat_idx[:, k, :], scatter_i[:, bass.ds(g * TILES, TILES)])\
                        .then_inc(s["a_idx"], 1)
                    pool.wait_ge(s["a_idx"], g + 1)
                    pool.wait_ge(s["a_mean"], g + 1)
                    stand(pool, "gate")
                    scatter(agg_d, scat_idx, mean, mean_out[k], k)

            steps(pool, EG, 0, scatter_means)

            for k in range(4):
                pool.wait_ge(x1_out[k], slot_count((NG - 1 - k) // 4 * 4 + k, k, 16))
                pool.wait_ge(o2_out[k], slot_count((NG - 1 - k) // 4 * 4 + k, k, 16))
            stand(pool, "gate")

            def layer1_rows(g, k):
                if inside(g, EG):
                    wait(pool, s["e_T"], g - 1)
                    wait(pool, s["e_z"], g - 3)
                    wait(pool, gathered[k], slot_count(g, k, 128, 1))
                    stand(pool, "gate")
                    nc.gpsimd.tensor_copy(src_idx[:, k, :], src_i[:, bass.ds(g * TILES, TILES)])\
                        .then_inc(s["e_idx"], 1)
                    nc.gpsimd.tensor_copy(dst_idx[:, k, :], gather_i[:, bass.ds(g * TILES, TILES)])\
                        .then_inc(s["e_idx"], 1)
                    pool.wait_ge(s["e_idx"], g * 2 + 2)
                    stand(pool, "gate")
                    gather(x1_d, src_idx, xs, k, k % 2, gathered[k])
                    gather(x1_d, dst_idx, xd, k, k, gathered[k])
                h, m = g - 4, k
                if inside(h, EG):
                    wait(pool, o3_out[m], slot_count(h, m, 64, 1))
                    stand(pool, "gate")
                    nc.gpsimd.tensor_copy(out_idx[:, m, :], scatter_i[:, bass.ds(h * TILES, TILES)])\
                        .then_inc(s["e_idx2"], 1)
                    pool.wait_ge(s["e_idx2"], h + 1)
                    pool.wait_ge(s["e_out"], h + 1)
                    stand(pool, "gate")
                    scatter(out, out_idx, o3, o3_out[m], m)

            steps(pool, EG, 4, layer1_rows)
            for k in range(4):
                pool.wait_ge(o3_out[k], slot_count((EG - 1 - k) // 4 * 4 + k, k, 64))

        @block.scalar
        def _(act):
            act.wait_ge(s["zeros_set"], 1)
            for n in range(NODES // ZSTEP + 1):
                if (n + 1) * ZSTEP > NODES:
                    act.wait_ge(s["zeroed"], 16 * n)
                base = min(n * ZSTEP, NODES - ZSTEP)
                act.dma_start(agg_d[base:base + ZSTEP, :].rearrange("(p a b) f -> p a (b f)", p=P, b=8),
                              zeros[:, :].unsqueeze(1).to_broadcast((P, ZROWS // 8, 8 * P)))\
                    .then_inc(s["zeroed"], 16)
            act.wait_ge(s["setup_v"], 9)
            act.dma_start(same_d.rearrange("(p c) -> p c", p=P), same_bf[:, :]).then_inc(s["masks_out"], 16)
            act.dma_start(reset_d.rearrange("(p c) -> p c", p=P), reset_bf[:, :]).then_inc(s["masks_out"], 16)
            act.wait_ge(s["setup_v"], 14)
            act.dma_start(rcount_d.rearrange("(p c) -> p c", p=P), rcount_r[:, :]).then_inc(s["rcount_out"], 16)
            act.wait_ge(s["setup_c"], 5)
            act.dma_start(bias_d.rearrange("(a k) f -> a k f", a=1),
                          bias_part[:, :, :, :].rearrange("a k b f -> a (k b) f")).then_inc(s["bias_out"], 16)

            def mean_evac(g, k):
                if inside(g, EG):
                    act.wait_ge(s["a_back"], g + 1)
                    wait(act, mean_out[k], slot_count(g, k, 64, 1))
                    for j in range(TILES):
                        col = bass.ds(g * TILES + j, 1)
                        i = nc.scalar.activation(mean[:, k, j, :], banks[2 + k % 2][:, j * P:(j + 1) * P], ACT.Copy,
                                                 scale=rcount_t[:, col])
                    i.then_inc(s["a_mean"], 1)

            steps(act, EG, 0, mean_evac)

            def node_act(g, k):
                if inside(g, NG):
                    act.wait_ge(s["n_T"], g + 1)
                    wait(act, s["n_h"], g - 1)
                    nc.scalar.activation(xT[:, k % 2, :], banks[0][:, :], ACT.Copy)
                    nc.scalar.activation(aT[:, k % 2, :], banks[1][:, :], ACT.Copy).then_inc(s["n_evac"], 1)
                h, m = g - 1, (k - 1) % 4
                if inside(h, NG):
                    act.wait_ge(s["n_h"], h + 1)
                    wait(act, s["n_y"], h - 1)
                    for c in range(2):
                        i = nc.scalar.activation(hT[:, m % 2, c, :], banks[2 + 2 * (m % 2) + c][:, :], ACT.Relu,
                                                 bias=b1_sb[:, c:c + 1])
                    i.then_inc(s["n_relu"], 1)
                h, m = g - 3, (k - 3) % 4
                if inside(h, NG):
                    act.wait_ge(s["n_aggr"], h + 1)
                    nc.scalar.activation(sd1[:, m, :], mv1[:, m, :, 1], ACT.Sqrt, bias=eps[:, :])\
                        .then_inc(s["n_sd"], 1)
                h, m = g - 5, (k - 5) % 4
                if inside(h, NG):
                    act.wait_ge(s["n_aggr2"], h + 1)
                    nc.scalar.activation(sd2[:, m, :], mv2[:, m, :, 1], ACT.Sqrt, bias=eps[:, :])\
                        .then_inc(s["n_sd2"], 1)
                h, m = g - 6, (k - 6) % 4
                if inside(h, NG):
                    act.wait_ge(s["n_nb2"], h + 1)
                    wait(act, o2_out[m], slot_count(h, m, 16, 1))
                    for j in range(TILES):
                        i = nc.scalar.activation(o2[:, m, j, :], z2[:, m, j, :], ACT.Identity,
                                                 bias=nb2[:, m, j:j + 1], scale=rs2[:, m, j:j + 1])
                    i.then_inc(s["n_out"], 1)

            steps(act, NG, 6, node_act)

            def edge_act(g, k):
                if inside(g, EG):
                    act.wait_ge(s["e_T"], g + 1)
                    wait(act, s["e_v"], g - 1)
                    nc.scalar.activation(xsT[:, k % 2, :], banks[0][:, :], ACT.Copy)
                    nc.scalar.activation(xdT[:, k % 2, :], banks[1][:, :], ACT.Copy).then_inc(s["e_evac"], 1)
                h, m = g - 2, (k - 2) % 4
                if inside(h, EG):
                    act.wait_ge(s["e_attnT"], h + 1)
                    wait(act, s["e_o"], h)
                    nc.scalar.activation(attnT[:, :], banks[6][:, :], ACT.Copy).then_inc(s["e_attnTs"], 1)
                h, m = g - 1, (k - 1) % 4
                if inside(h, EG):
                    act.wait_ge(s["e_q"], h + 1)
                    wait(act, s["e_qk"], h)
                    nc.scalar.activation(qT[:, :], banks[2][:, :], ACT.Identity, bias=qkvb_sb[:, 0:1])\
                        .then_inc(s["e_qT"], 1)
                    act.wait_ge(s["e_drop"], h + 1)
                    wait(act, s["e_acc"], h)
                    nc.scalar.activation(decay[:, :], drop[:, :], ACT.Exp).then_inc(s["e_decay"], 1)
                    act.wait_ge(s["e_rise"], h + 1)
                    nc.scalar.activation(prob[:, :], rise[:, :], ACT.Exp).then_inc(s["e_prob"], 1)
                h, m = g - 2, (k - 2) % 4
                if inside(h, EG):
                    act.wait_ge(s["e_aggr"], h + 1)
                    nc.scalar.activation(ln3[:, :], mv3[:, m % 2, :, 1], ACT.Ln, bias=eps[:, :]).then_inc(s["e_ln"], 1)
                    act.wait_ge(s["e_ln"], h + 1)
                    wait(act, s["e_out"], h - 1)
                    nc.scalar.activation(rs3[:, m % 2, :], ln3[:, :], ACT.Exp, scale=-0.5).then_inc(s["e_rs"], 1)
                h, m = g - 3, (k - 3) % 4
                if inside(h, EG):
                    act.wait_ge(s["e_nb"], h + 1)
                    wait(act, o3_out[m], slot_count(h, m, 64, 1))
                    for j in range(TILES):
                        i = nc.scalar.activation(o3[:, m, j, :], z3[:, m % 2, j, :], ACT.Identity,
                                                 bias=nb3[:, m % 2, j:j + 1], scale=rs3[:, m % 2, j:j + 1])
                    i.then_inc(s["e_out"], 1)

            steps(act, EG, 3, edge_act)

        @block.vector
        def _(dve):
            V = nc.vector
            done = [0, 0]

            def then(ins):
                done[0] += 1
                ins.then_inc(s["setup_v"], 1)
                dve.wait_ge(s["setup_v"], done[0])

            def thenc(ins):
                done[1] += 1
                ins.then_inc(s["setup_c"], 1)
                dve.wait_ge(s["setup_c"], done[1])

            V.memset(zeros[:, :], 0.0).then_inc(s["zeros_set"], 1)
            V.memset(attr_tail[:, :, :], 0.0).then_inc(s["zeros_set"], 1)
            V.memset(ones3[:, :], 1.0)
            V.memset(one1[:, :], 1.0)
            V.memset(start_row[:, :], 0.0)
            V.memset(mx[:, 0, 0:1], -FAR)
            V.memset(eps[:, :], EPS).then_inc(s["consts_set"], 1)
            dve.wait_ge(s["rows_in"], 32)
            dve.wait_ge(s["iota_done"], 1)
            dve.wait_ge(s["consts_set"], 1)
            then(V.tensor_copy(cur_rf[:, :], cur_r[:, :]))
            then(V.tensor_copy(prev_rf[:, :], prev_r[:, :]))
            then(V.tensor_tensor(same_r[:, :], cur_rf[:, :], prev_rf[:, :], ALU.is_equal))
            then(V.tensor_copy(same_bf[:, :], same_r[:, :]))
            then(V.tensor_scalar(reset_bf[:, :], same_r[:, :], 2.0 * FAR, -FAR, ALU.mult, ALU.add))
            then(V.tensor_copy(edge_no[:, :], edge_no_i[:, :]))
            then(V.tensor_tensor(first_r[:, :], edge_no[:, :], same_r[:, :], ALU.mult))
            then(V.tensor_tensor(first_r[:, :], edge_no[:, :], first_r[:, :], ALU.subtract))
            then(V.tensor_tensor_scan(start_r[:, :], first_r[:, :], first_r[:, :], 0.0, ALU.max, ALU.max))
            dve.wait_ge(s["setup_t"], 1)
            then(V.tensor_tensor_scan(start_row[:, 1:P + 1], banks[7][0:1, 0:P], start_row[:, 0:1].to_broadcast((1, P)),
                                      0.0, ALU.max, ALU.max))
            dve.wait_ge(s["setup_t"], 2)
            then(V.tensor_copy(start_in[:, :], banks[6][:, 0:1]))
            then(V.tensor_scalar(count_r[:, :], start_r[:, :], start_in[:, :], None, ALU.max))
            then(V.scalar_tensor_tensor(count_r[:, :], edge_no[:, :], 1.0, count_r[:, :], ALU.add, ALU.subtract))
            then(V.reciprocal(rcount_r[:, :], count_r[:, :]))
            dve.wait_ge(s["tiles_in"], 48)
            then(V.tensor_copy(dst_f[:, :], dst_i[:, :]))
            then(V.tensor_copy(next_f[:, :], next_i[:, :]))
            then(V.tensor_tensor(inner_f[:, :], dst_f[:, :], next_f[:, :], ALU.is_equal))
            then(V.scalar_tensor_tensor(scatter_f[:, :], inner_f[:, :], SKIP, dst_f[:, :], ALU.mult, ALU.add))
            then(V.tensor_copy(scatter_i[:, :], scatter_f[:, :]))
            then(V.tensor_scalar(gather_i[:, :], dst_f[:, :], float(NODES - 1), None, ALU.min))
            dve.wait_ge(s["weights_in"], 16 * 12)
            thenc(V.tensor_copy(bias_part[:, 0, :, :], bias_row[:, :, :]))
            thenc(V.tensor_tensor(bias_left[:, 0, :, :], bias_row[:, :, :], bias_part[:, 0, :, :], ALU.subtract))
            thenc(V.tensor_copy(bias_part[:, 1, :, :], bias_left[:, 0, :, :]))
            thenc(V.tensor_tensor(bias_left[:, 1, :, :], bias_left[:, 0, :, :], bias_part[:, 1, :, :], ALU.subtract))
            thenc(V.tensor_copy(bias_part[:, 2, :, :], bias_left[:, 1, :, :]))
            dve.wait_ge(s["setup_t"], 4)
            for b in range(2):
                V.tensor_copy(rcount_t[:, b * (ET // 2):(b + 1) * (ET // 2)], banks[4 + b][:, 0:ET // 2])\
                    .then_inc(s["setup_c"], 1)

            def sums(g, k):
                if inside(g, EG):
                    dve.wait_ge(s["a_T"], g + 1)
                    dve.wait_ge(same_in[k], slot_count(g, k, 16))
                    wait(dve, s["a_back"], g - 3)
                    wait(dve, s["a_scan"], g)
                    start = 0.0 if isinstance(g, int) and g == 0 else sumT[:, (k - 1) % 4, GROUP - 1:GROUP]
                    V.tensor_tensor_scan(sumT[:, k, :], same_sb[:, k, :], banks[k % 2][:, :], start,
                                         ALU.mult, ALU.add).then_inc(s["a_scan"], 1)

            steps(dve, EG, 0, sums)

            def norm_stats(z, stats, mv, stats_done, mv_done, h):
                for j in range(TILES):
                    i = V.bn_stats(stats[:, j, :], z[:, j, :])
                i.then_inc(stats_done, 1)
                dve.wait_ge(stats_done, h + 1)
                stand(dve, "gate_dve")
                for j in range(TILES):
                    i = V.bn_aggr(mv[:, j, :], stats[:, j, :])
                i.then_inc(mv_done, 1)

            def node_dve(g, k):
                h, m = g - 2, (k - 2) % 4
                if inside(h, NG):
                    dve.wait_ge(s["n_y"], h + 1)
                    V.tensor_tensor(z1[:, m, :, :].rearrange("p j f -> p (j f)"), banks[6 + m % 2][:, :],
                                    xn[:, m, :, :].rearrange("p j f -> p (j f)"), ALU.add).then_inc(s["n_z"], 1)
                    dve.wait_ge(s["n_z"], h + 1)
                    norm_stats(z1[:, m], st1[:, m % 2], mv1[:, m], s["n_stats"], s["n_aggr"], h)
                h, m = g - 3, (k - 3) % 4
                if inside(h, NG):
                    dve.wait_ge(s["n_sd"], h + 1)
                    V.reciprocal(rs1[:, m, :], sd1[:, m, :]).then_inc(s["n_rs"], 1)
                    dve.wait_ge(s["n_rs"], h + 1)
                    wait(dve, x1_out[m], slot_count(h, m, 16, 1))
                    for j in range(TILES):
                        i = V.tensor_scalar(x1[:, m, j, :], z1[:, m, j, :], mv1[:, m, j, 0:1], rs1[:, m, j:j + 1],
                                            ALU.subtract, ALU.mult)
                    i.then_inc(s["n_x1"], 1)
                h, m = g - 4, (k - 4) % 4
                if inside(h, NG):
                    dve.wait_ge(s["n_x1"], h + 1)
                    wait(dve, s["n_out"], h - 3)
                    V.tensor_tensor(z2[:, m, :, :], x1[:, m, :, :],
                                    outb_bc[:, :].unsqueeze(1).to_broadcast((P, TILES, P)), ALU.add)\
                        .then_inc(s["n_z2"], 1)
                    dve.wait_ge(s["n_z2"], h + 1)
                    norm_stats(z2[:, m], st2[:, m % 2], mv2[:, m], s["n_stats2"], s["n_aggr2"], h)
                h, m = g - 5, (k - 5) % 4
                if inside(h, NG):
                    dve.wait_ge(s["n_sd2"], h + 1)
                    V.reciprocal(rs2[:, m, :], sd2[:, m, :]).then_inc(s["n_rs2"], 1)
                    dve.wait_ge(s["n_rs2"], h + 1)
                    V.scalar_tensor_tensor(nb2[:, m, :], mv2[:, m, :, 0], -1.0, rs2[:, m, :], ALU.mult, ALU.mult)\
                        .then_inc(s["n_nb2"], 1)

            steps(dve, NG, 5, node_dve)

            def edge_dve(g, k):
                h, m = g - 2, (k - 2) % 4
                if inside(h, EG):
                    dve.wait_ge(s["e_back"], h + 1)
                    V.reciprocal(rden[:, :, :].rearrange("p j h -> p (j h)"), banks[7][:, 0:TILES * HEADS])\
                        .then_inc(s["e_rden"], 1)
                    dve.wait_ge(s["e_rden"], h + 1)
                    wait(dve, s["e_attnT"], h)
                    V.tensor_tensor(attn[:, :, :].rearrange("p j (h d) -> p (j h) d", d=HD),
                                    banks[6][:, :].rearrange("p (a d) -> p a d", d=HD),
                                    rden[:, :, :].rearrange("p j h -> p (j h)").unsqueeze(2)
                                    .to_broadcast((P, TILES * HEADS, HD)), ALU.mult).then_inc(s["e_attn"], 1)
                h, m = g - 1, (k - 1) % 4
                if inside(h, EG):
                    dve.wait_ge(s["e_qT"], h + 1)
                    dve.wait_ge(s["e_k"], h + 1)
                    wait(dve, s["e_s"], h)
                    V.scalar_tensor_tensor(qk[:, :], banks[3][:, :], qkvb_sb[:, 1:2], qT[:, :], ALU.add, ALU.mult)\
                        .then_inc(s["e_qk"], 1)
                h, m = g - 2, (k - 2) % 4
                if inside(h, EG):
                    dve.wait_ge(s["e_o"], h + 1)
                    wait(dve, s["e_out"], h - 1)
                    V.tensor_tensor(z3[:, m % 2, :, :].rearrange("p j f -> p (j f)"), banks[7][:, :],
                                    xd[:, m, :, :].rearrange("p j f -> p (j f)"), ALU.add).then_inc(s["e_z"], 1)
                    dve.wait_ge(s["e_z"], h + 1)
                    norm_stats(z3[:, m % 2], st3, mv3[:, m % 2], s["e_stats"], s["e_aggr"], h)
                h, m = g - 1, (k - 1) % 4
                if inside(h, EG):
                    dve.wait_ge(s["e_s"], h + 1)
                    dve.wait_ge(reset_in[m], slot_count(h, m, 16))
                    wait(dve, s["e_carry"], h)
                    V.tensor_tensor_scan(mx[:, m, 1:GROUP + 1], reset_sb[:, m, :], banks[5][:, :],
                                         mx[:, m, 0:1], ALU.min, ALU.max).then_inc(s["e_mx"], 1)
                    dve.wait_ge(s["e_mx"], h + 1)
                    V.tensor_copy(mx[:, (m + 1) % 4, 0:1], mx[:, m, GROUP:GROUP + 1]).then_inc(s["e_carry"], 1)
                    V.tensor_tensor(keep[:, :], mx[:, m, 0:GROUP], reset_sb[:, m, :], ALU.min)\
                        .then_inc(s["e_keep"], 1)
                    dve.wait_ge(s["e_keep"], h + 1)
                    wait(dve, s["e_decay"], h)
                    V.tensor_tensor(drop[:, :], keep[:, :], mx[:, m, 1:GROUP + 1], ALU.subtract)\
                        .then_inc(s["e_drop"], 1)
                    wait(dve, s["e_prob"], h)
                    V.tensor_tensor(rise[:, :], banks[5][:, :], mx[:, m, 1:GROUP + 1], ALU.subtract)\
                        .then_inc(s["e_rise"], 1)
                h, m = g - 2, (k - 2) % 4
                if inside(h, EG):
                    dve.wait_ge(s["e_rs"], h + 1)
                    V.scalar_tensor_tensor(nb3[:, m % 2, :], mv3[:, m % 2, :, 0], -1.0, rs3[:, m % 2, :],
                                           ALU.mult, ALU.mult).then_inc(s["e_nb"], 1)
                h, m = g - 1, (k - 1) % 4
                if inside(h, EG):
                    first = isinstance(h, int) and h == 0
                    dve.wait_ge(s["e_prob"], h + 1)
                    dve.wait_ge(s["e_v"], h + 1)
                    V.scalar_tensor_tensor(pv[:, :], banks[4][:, :], qkvb_sb[:, 2:3], prob[:, :], ALU.add, ALU.mult)\
                        .then_inc(s["e_pv"], 1)
                    dve.wait_ge(s["e_decay"], h + 1)
                    wait(dve, s["e_den"], h)
                    wait(dve, s["e_back"], h - 1)
                    V.tensor_tensor_scan(den[:, m % 2, :], decay[:, :], prob[:, :],
                                         0.0 if first else den[:, (m + 1) % 2, GROUP - 1:GROUP],
                                         ALU.mult, ALU.add).then_inc(s["e_den"], 1)
                    dve.wait_ge(s["e_pv"], h + 1)
                    wait(dve, s["e_acc"], h)
                    V.tensor_tensor_scan(acc[:, m % 2, :], decay[:, :], pv[:, :],
                                         0.0 if first else acc[:, (m + 1) % 2, GROUP - 1:GROUP],
                                         ALU.mult, ALU.add).then_inc(s["e_acc"], 1)

            steps(dve, EG, 2, edge_dve)

        @block.tensor
        def _(pe):
            T = nc.tensor
            pe.wait_ge(s["weights_in"], 16 * 12)
            pe.wait_ge(s["consts_set"], 1)
            pe.wait_ge(s["setup_v"], 9)
            T.transpose(banks[7][0:1, 0:P], start_r[:, EROW - 1:EROW], ident[:, :]).then_inc(s["setup_t"], 1)
            pe.wait_ge(s["setup_v"], 10)
            T.matmul(banks[6][:, 0:1], start_row[:, 0:P], one1[:, :], start=True, stop=True)\
                .then_inc(s["setup_t"], 1)
            pe.wait_ge(s["rcount_in"], 16)
            for b in range(2):
                T.transpose(banks[4 + b][:, 0:ET // 2], rcount_l[:, b, :], ident[0:ET // 2, 0:ET // 2])\
                    .then_inc(s["setup_t"], 1)
            pe.wait_ge(s["attr_tail_in"], 32)

            def edge_sums(g, k):
                if inside(g, EG):
                    last = isinstance(g, int) and g == EG - 1
                    if not last:
                        pe.wait_ge(attr_in[k], slot_count(g, k, 16))
                    wait(pe, s["a_scan"], g - 1)
                    for j in range(TILES):
                        src = attr_tail[:, j, :] if last else attr_sb[:, k, j, :]
                        i = T.transpose(banks[k % 2][:, j * P:(j + 1) * P], src, ident[:, :])
                    i.then_inc(s["a_T"], 1)
                h, m = g - 1, (k - 1) % 4
                if inside(h, EG):
                    pe.wait_ge(s["a_scan"], h + 1)
                    wait(pe, s["a_mean"], h - 1)
                    for j in range(TILES):
                        i = T.transpose(banks[2 + m % 2][:, j * P:(j + 1) * P], sumT[:, m, j * P:(j + 1) * P],
                                        ident[:, :])
                    i.then_inc(s["a_back"], 1)

            steps(pe, EG, 1, edge_sums)
            pe.wait_ge(s["a_mean"], EG)
            pe.wait_ge(s["setup_c"], 7)
            pe.wait_ge(s["bias_in"], 16)

            def node_pe(g, k):
                if inside(g, NG):
                    pe.wait_ge(node_in[k], slot_count(g, k, 32))
                    wait(pe, s["n_evac"], g)
                    for src, bank in ((xn, 0), (an, 1)):
                        for j in range(TILES):
                            i = T.transpose(banks[bank][:, j * P:(j + 1) * P], src[:, k, j, :], ident[:, :])
                    i.then_inc(s["n_T"], 1)
                h, m = g - 1, (k - 1) % 4
                if inside(h, NG):
                    pe.wait_ge(s["n_evac"], h + 1)
                    wait(pe, s["n_relu"], h - 1)
                    for c in range(2):
                        bank = banks[2 + 2 * (m % 2) + c]
                        T.matmul(bank[:, :], w1_sb[:, 0, c * P:(c + 1) * P], xT[:, m % 2, :], start=True, stop=False)
                        i = T.matmul(bank[:, :], w1_sb[:, 1, c * P:(c + 1) * P], aT[:, m % 2, :],
                                     start=False, stop=True)
                    i.then_inc(s["n_h"], 1)
                h, m = g - 2, (k - 2) % 4
                if inside(h, NG):
                    pe.wait_ge(s["n_relu"], h + 1)
                    wait(pe, s["n_z"], h - 1)
                    bank = banks[6 + m % 2]
                    T.matmul(bank[:, :], ones3[:, :], bias3[:, 0, :].unsqueeze(1).to_broadcast((3, TILES, P)),
                             start=True, stop=False)
                    for j in range(TILES):
                        for c in range(2):
                            i = T.matmul(bank[:, j * P:(j + 1) * P], hT[:, m % 2, c, j * P:(j + 1) * P],
                                         w2_sb[:, c, :], start=False, stop=(c == 1 and j == TILES - 1))
                    i.then_inc(s["n_y"], 1)

            steps(pe, NG, 2, node_pe)
            pe.wait_ge(s["n_z"], NG)
            pe.wait_ge(s["n_relu"], NG)

            def edge_pe(g, k):
                h, m = g - 2, (k - 2) % 4
                if inside(h, EG):
                    pe.wait_ge(s["e_acc"], h + 1)
                    wait(pe, s["e_attnTs"], h)
                    wait(pe, s["e_z"], h)
                    for j in range(TILES):
                        T.transpose(banks[6][:, j * P:(j + 1) * P], acc[:, m % 2, j * P:(j + 1) * P], ident[:, :])
                    for j in range(TILES):
                        i = T.matmul(banks[7][:, j * HEADS:(j + 1) * HEADS], den[:, m % 2, j * P:(j + 1) * P],
                                     head_pick[:, :], start=True, stop=True)
                    i.then_inc(s["e_back"], 1)
                if inside(g, EG):
                    pe.wait_ge(gathered[k], slot_count(g, k, 128))
                    wait(pe, s["e_evac"], g)
                    for j in range(TILES):
                        T.transpose(banks[0][:, j * P:(j + 1) * P], xs[:, k % 2, j, :], ident[:, :])
                    for j in range(TILES):
                        i = T.transpose(banks[1][:, j * P:(j + 1) * P], xd[:, k, j, :], ident[:, :])
                    i.then_inc(s["e_T"], 1)
                if inside(h, EG):
                    pe.wait_ge(s["e_attn"], h + 1)
                    for j in range(TILES):
                        i = T.transpose(banks[6][:, j * P:(j + 1) * P], attn[:, j, :], ident[:, :])
                    i.then_inc(s["e_attnT"], 1)
                h, m = g - 1, (k - 1) % 4
                if inside(h, EG):
                    pe.wait_ge(s["e_evac"], h + 1)
                    wait(pe, s["e_qT"], h)
                    T.matmul(banks[2][:, :], qkvw_sb[:, 0:P], xdT[:, m % 2, :], start=True, stop=True)\
                        .then_inc(s["e_q"], 1)
                    wait(pe, s["e_qk"], h)
                    T.matmul(banks[3][:, :], qkvw_sb[:, P:2 * P], xsT[:, m % 2, :], start=True, stop=True)\
                        .then_inc(s["e_k"], 1)
                    wait(pe, s["e_pv"], h)
                    T.matmul(banks[4][:, :], qkvw_sb[:, 2 * P:3 * P], xsT[:, m % 2, :], start=True, stop=True)\
                        .then_inc(s["e_v"], 1)
                h, m = g - 2, (k - 2) % 4
                if inside(h, EG):
                    pe.wait_ge(s["e_attnTs"], h + 1)
                    T.matmul(banks[7][:, :], ones3[:, :], bias3[:, 1, :].unsqueeze(1).to_broadcast((3, TILES, P)),
                             start=True, stop=False)
                    for j in range(TILES):
                        i = T.matmul(banks[7][:, j * P:(j + 1) * P], attnT[:, j * P:(j + 1) * P], outw_sb[:, :],
                                     start=False, stop=(j == TILES - 1))
                    i.then_inc(s["e_o"], 1)
                h, m = g - 1, (k - 1) % 4
                if inside(h, EG):
                    pe.wait_ge(s["e_qk"], h + 1)
                    wait(pe, s["e_rise"], h)
                    T.matmul(banks[5][:, :], head_sum[:, :], qk[:, :], start=True, stop=True).then_inc(s["e_s"], 1)

            steps(pe, EG, 2, edge_pe)


def kernel(x, src, dst, edge_attr_128, L0_gnn_W1, L0_gnn_b1, L0_gnn_W2, L0_gnn_b2, L1_gnn_qkv_w, L1_gnn_qkv_b,
           L1_gnn_out_w, L1_gnn_out_b):
    import numpy as np
    import concourse.bacc as bacc
    from concourse.bass_utils import run_bass_kernel_spmd as run

    src, dst = np.asarray(src), np.asarray(dst)
    pad = EPAD - EDGES
    dst_p = np.concatenate([dst, np.full(pad, PAD_NODE, dst.dtype)])
    next_p = np.concatenate([dst[1:], np.full(pad + 1, PAD_NODE, dst.dtype)])
    prev_p = np.concatenate([np.full(1, -1, dst.dtype), dst_p[:-1]])
    src_p = np.concatenate([src, np.zeros(pad, src.dtype)])
    head = np.arange(P) // HD
    ins = {
        "x": x, "attr": edge_attr_128,
        "dst_tile": dst_p.reshape(ET, P).T, "next_tile": next_p.reshape(ET, P).T, "src_tile": src_p.reshape(ET, P).T,
        "dst_row": dst_p.reshape(P, EROW), "prev_row": prev_p.reshape(P, EROW),
        "w1": L0_gnn_W1, "b1": np.asarray(L0_gnn_b1).reshape(2, P).T,
        "w2": L0_gnn_W2, "b2": np.asarray(L0_gnn_b2).reshape(1, P),
        "qkv_wT": np.asarray(L1_gnn_qkv_w).T, "qkv_b": np.asarray(L1_gnn_qkv_b).reshape(3, P).T,
        "out_wT": np.asarray(L1_gnn_out_w).T, "out_b": np.asarray(L1_gnn_out_b).reshape(1, P),
        "ident_c": np.eye(P, dtype=np.float32),
        "head_sum_c": (head[:, None] == head[None, :]).astype(np.float32) * np.float32(HD ** -0.5),
        "head_pick_c": (np.arange(P)[:, None] == HD * np.arange(HEADS)[None, :]).astype(np.float32),
    }
    ins = {k: np.ascontiguousarray(v) for k, v in ins.items()}
    nc = bacc.Bacc("TRN2", target_bir_lowering=False, num_devices=1)
    args = {k: nc.dram_tensor(k, v.shape, mybir.dt.from_np(v.dtype), kind="ExternalInput").ap()
            for k, v in ins.items()}
    out = nc.dram_tensor("out", (NODES, P), F32, kind="ExternalOutput").ap()
    build(nc, out=out, **args)
    r = run(nc, [ins], core_ids=[0])
    return r.results[0]["out"]
```

```python
from contextlib import ExitStack

import concourse.bass as bass
from concourse import mybir

F32 = mybir.dt.float32
BF16 = mybir.dt.bfloat16
I32 = mybir.dt.int32
ALU = mybir.AluOpType
ACT = mybir.ActivationFunctionType

P = 128
NODES = 50000
EDGES = 25000
TILES = 4
GROUP = TILES * P
NG = -(-NODES // GROUP)
EG = -(-EDGES // GROUP)
EPAD = EG * GROUP
ET = EPAD // P
EROW = EPAD // P
HID = 256
HEADS = 8
HD = P // HEADS
EPS = 1e-5
FAR = 1.0e30
PAD_NODE = NODES
SKIP = 65536.0
ZROWS = -(-NODES // (EG * P))
ZSTEP = P * ZROWS


def build(nc, x, attr, dst_tile, next_tile, src_tile, dst_row, prev_row, first_dst, last_dst, w1, b1, w2, b2, qkv_wT, qkv_b, out_wT,
          out_b, ident_c, head_sum_c, out):
    table_d = nc.dram_tensor("table_scratch", (NODES, P), F32).ap()
    same_d = nc.dram_tensor("same_scratch", (EPAD,), BF16).ap()
    reset_d = nc.dram_tensor("reset_scratch", (EPAD,), BF16).ap()
    rcount_d = nc.dram_tensor("rcount_scratch", (EPAD,), F32).ap()
    bias_d = nc.dram_tensor("bias_scratch", (6, P), BF16).ap()

    ctx = ExitStack()
    with ctx:
        def sb(name, shape, dt=F32):
            return ctx.enter_context(nc.sbuf_tensor(name, shape, dt))

        def sem(name):
            return ctx.enter_context(nc.semaphore(name))

        ident = sb("ident", [P, P])
        head_sum = sb("head_sum", [P, P])
        w1_sb = sb("w1_sb", [P, 2, HID])
        w2_sb = sb("w2_sb", [P, 2, P])
        qkvw_sb = sb("qkvw_sb", [P, 3 * P])
        outw_sb = sb("outw_sb", [P, P])
        b1_sb = sb("b1_sb", [P, 2])
        qkvb_sb = sb("qkvb_sb", [P, 3])
        outb_bc = sb("outb_bc", [P, P])
        bias_row = sb("bias_row", [1, 2, P])
        bias_left = sb("bias_left", [1, 2, 2, P])
        bias_part = sb("bias_part", [1, 3, 2, P], BF16)
        bias3 = sb("bias3", [3, 2, P], BF16)
        ones3 = sb("ones3", [3, P], BF16)
        one1 = sb("one1", [1, 1])
        eps = sb("eps", [P, 1])
        zeros = sb("zeros", [P, 4 * P])

        src_i = sb("src_i", [P, ET], I32)
        scatter_i = sb("scatter_i", [P, ET], I32)
        gather_i = sb("gather_i", [P, ET], I32)
        rcount_t = sb("rcount_t", [P, ET])
        start_row = sb("start_row", [1, P + 1])
        start_in = sb("start_in", [P, 1])
        needs = sb("needs", [P, 3])
        needs_i = sb("needs_i", [1, 3 * P], I32)
        need_scattered = needs_i[:, 0:NG]
        need_stored = needs_i[:, P:P + EG]
        need_zeroed = needs_i[:, 2 * P:2 * P + EG]

        rows = sb("rows", [P, EG, TILES, P])
        attr_sb = sb("attr_sb", [P, 4, TILES, P])
        attr_tail = sb("attr_tail", [P, TILES, P])
        same_sb = sb("same_sb", [P, 4, GROUP], BF16)
        sumT = sb("sumT", [P, 4, GROUP])

        xn = sb("xn", [P, 4, TILES, P])
        an = sb("an", [P, 4, TILES, P])
        xT = sb("xT", [P, 2, GROUP])
        aT = sb("aT", [P, 2, GROUP])
        hT = sb("hT", [P, 2, 2, GROUP])
        x1 = sb("x1", [P, 4, TILES, P])
        o2 = sb("o2", [P, 4, TILES, P])
        st1 = sb("st1", [P, 2, TILES, 6])
        mv1 = sb("mv1", [P, 4, TILES, 2])
        sd1 = sb("sd1", [P, 4, TILES])
        rs1 = sb("rs1", [P, 4, TILES])
        st2 = sb("st2", [P, 2, TILES, 6])
        mv2 = sb("mv2", [P, 4, TILES, 2])
        sd2 = sb("sd2", [P, 4, TILES])
        rs2 = sb("rs2", [P, 4, TILES])
        nb2 = sb("nb2", [P, 4, TILES])

        def lend(tensor, n, cols, dt=F32, parts=P):
            flat = tensor[:, :, :, :].rearrange("p a b c -> p (a b c)")[0:parts, n * EROW:n * EROW + cols]
            return flat if dt == F32 else flat.bitcast(dt)

        cur_r, prev_r = lend(hT, 0, EROW, I32), lend(hT, 1, EROW, I32)
        cur_rf, prev_rf, same_r = (lend(hT, n, EROW) for n in (2, 3, 4))
        edge_no_i = lend(hT, 5, EROW, I32)
        edge_no, first_r, start_r, count_r = (lend(hT, n, EROW) for n in (6, 7, 8, 9))
        rcount_r = lend(x1, 0, EROW)
        dst_i, next_i = lend(x1, 1, EROW, I32), lend(x1, 2, EROW, I32)
        dst_f, next_f, inner_f, scatter_f = (lend(x1, n, EROW) for n in (3, 4, 5, 6))
        first_i, first_f, first_c = lend(x1, 7, EG, I32, NG), lend(x1, 8, EG, parts=NG), lend(x1, 9, EG, parts=NG)
        edge_end_i, edge_end = lend(o2, 0, 1, I32), lend(o2, 1, 1)
        last_i, last_f = lend(o2, 2, 1, I32, EG), lend(o2, 3, 1, parts=EG)
        base_i, base_f, base_c = lend(o2, 4, NG, I32, EG), lend(o2, 5, NG, parts=EG), lend(o2, 6, NG, parts=EG)
        zbase_i, zbase_f, zbase_c = lend(o2, 7, EG, I32, EG), lend(o2, 8, EG, parts=EG), lend(o2, 9, EG, parts=EG)
        same_bf = sb("same_bf", [P, EROW], BF16)
        reset_bf = sb("reset_bf", [P, EROW], BF16)
        rcount_l = xn[0:ET // 2, 0, 0:2, :]

        src_idx = sb("src_idx", [P, 4, TILES], I32)
        out_idx = sb("out_idx", [P, 4, TILES], I32)
        xs = attr_sb
        reset_sb = same_sb
        xsT, xdT = xT, aT
        qT, keep = hT[:, 0, 0, :], hT[:, 0, 1, :]
        qk = hT[:, 1, :, :]
        vT = o2[:, 0:2, :, :].rearrange("p a j f -> p a (j f)")
        drop = o2[:, 2, :, :].rearrange("p j f -> p (j f)")
        den, acc = sumT[:, 0:2, :], sumT[:, 2:4, :]
        attn, attnT = x1[:, 0, :, :], x1[:, 1, :, :].rearrange("p j f -> p (j f)")
        rise, decay = (x1[:, n, :, :].rearrange("p j f -> p (j f)") for n in (2, 3))
        prob, pv = sb("prob", [P, GROUP]), sb("pv", [P, GROUP])
        mx = sb("mx", [P, 4, GROUP + 1])
        rden = sb("rden", [P, TILES, HEADS])
        z3, o3 = xn, an
        xd = sb("xd", [P, 2, GROUP])
        st3 = sb("st3", [P, TILES, 6])
        mv3 = sb("mv3", [P, 4, TILES, 2])
        sd3 = sb("sd3", [P, 4, TILES])
        rs3 = sb("rs3", [P, 4, TILES])
        nb3 = sb("nb3", [P, 4, TILES])

        banks = [ctx.enter_context(nc.psum_tensor(f"bank{i}", [P, GROUP], F32)) for i in range(8)]

        names = """weights_in rows_in tiles_in attr_tail_in zeroed gate_act bias_out bias_in masks_out rcount_out rcount_in
            consts_set zeros_set iota_done gate_sp gate_dve setup_v setup_t setup_c gate
            a_T a_scan a_back a_mean
            n_T n_evac n_h n_relu n_y n_z n_stats n_aggr n_sd n_rs n_x1 n_z2 n_stats2 n_aggr2 n_sd2 n_rs2 n_nb2 n_out needs_made
            e_idx e_idx2 e_xd e_T e_evac e_q e_k e_v e_qT e_vT e_qk e_s e_mx e_keep e_drop e_rise e_decay e_prob e_pv e_den e_acc
            e_back e_rden e_attn e_attnT e_attnTs e_o e_z e_stats e_aggr e_sd e_rs e_nb e_out e_carry scattered stored needs_in""".split()
        s = {n: sem(n) for n in names}
        attr_in = [sem(f"attr_in{k}") for k in range(4)]
        zero_out = [sem(f"zero_out{k}") for k in range(4)]
        dst_in = [sem(f"dst_in{k}") for k in range(4)]
        same_in = [sem(f"same_in{k}") for k in range(4)]
        mean_out = [sem(f"mean_out{k}") for k in range(4)]
        node_in = [sem(f"node_in{k}") for k in range(4)]
        x1_out = [sem(f"x1_out{k}") for k in range(4)]
        o2_out = [sem(f"o2_out{k}") for k in range(4)]
        reset_in = [sem(f"reset_in{k}") for k in range(4)]
        gathered = [sem(f"gathered{k}") for k in range(4)]
        o3_out = [sem(f"o3_out{k}") for k in range(4)]

        def steps(eng, total, lag, body, begin=0):
            first = -(-(4 + lag) // 4) * 4
            last = (total - 1) // 4 * 4
            for g in range(begin, first):
                body(g, g % 4, g // 4)
            with eng.Fori(first // 4, last // 4) as i:
                for k in range(4):
                    body(i * 4 + k, k, i)
            for g in range(last, total + lag):
                body(g, g % 4, g // 4)

        def inside(g, total):
            return not isinstance(g, int) or 0 <= g < total

        def wait(eng, semaphore, value):
            if not isinstance(value, int) or value > 0:
                eng.wait_ge(semaphore, value)

        def slot_count(g, k, per, back=0):
            if isinstance(g, int):
                return ((g - k) // 4 + 1 - back) * per
            return (g - k) * (per // 4) + (1 - back) * per

        def node_base(g):
            return min(g * GROUP, NODES - GROUP) if isinstance(g, int) else g * GROUP

        def node_rows(t, g):
            return t[bass.ds(node_base(g), GROUP), :].rearrange("(p j) f -> p j f", j=TILES)

        def stand(eng, gate):
            eng.sem_inc(s[gate], 1)

        def all_uses(semaphores, total, per):
            return [(semaphores[k], slot_count((total - 1 - k) // 4 * 4 + k, k, per)) for k in range(4)]

        block = ctx.enter_context(nc.Block())

        @block.sync
        def _(sp):
            for t, src in ((cur_r, dst_row), (prev_r, prev_row)):
                sp.dma_start(t, src).then_inc(s["rows_in"], 16)
            for t, src in ((dst_i, dst_tile), (next_i, next_tile), (src_i[:, :], src_tile)):
                sp.dma_start(t, src).then_inc(s["tiles_in"], 16)
            sp.dma_start(first_i, first_dst.to_broadcast((NG, EG))).then_inc(s["needs_in"], 16)
            sp.dma_start(last_i, last_dst).then_inc(s["needs_in"], 16)
            for t, src in (
                (ident[:, :], ident_c), (head_sum[:, :], head_sum_c),
                (w1_sb[:, :, :], w1.rearrange("(c p) h -> p c h", p=P)),
                (w2_sb[:, :, :], w2.rearrange("(c p) h -> p c h", p=P)),
                (qkvw_sb[:, :], qkv_wT), (outw_sb[:, :], out_wT), (b1_sb[:, :], b1), (qkvb_sb[:, :], qkv_b),
                (outb_bc[:, :], out_b.to_broadcast((P, P))),
                (bias_row[:, 0, :], b2), (bias_row[:, 1, :], out_b),
            ):
                sp.dma_start(t, src).then_inc(s["weights_in"], 16)
            sp.wait_ge(s["zeros_set"], 2)
            full = (EDGES - (EG - 1) * GROUP) // P
            rest = EDGES - (EG - 1) * GROUP - full * P
            tail = attr[(EG - 1) * GROUP:, :]
            sp.dma_start(attr_tail[:, 0:full, :], tail[0:full * P, :].rearrange("(j p) f -> p j f", p=P))\
                .then_inc(s["attr_tail_in"], 16)
            sp.dma_start(attr_tail[0:rest, full, :], tail[full * P:full * P + rest, :])\
                .then_inc(s["attr_tail_in"], 16)
            sp.wait_ge(s["setup_v"], 9)
            sp.dma_start(same_d.rearrange("(p c) -> p c", p=P), same_bf[:, :]).then_inc(s["masks_out"], 16)
            sp.dma_start(reset_d.rearrange("(p c) -> p c", p=P), reset_bf[:, :]).then_inc(s["masks_out"], 16)
            sp.wait_ge(s["setup_v"], 14)
            sp.dma_start(rcount_d.rearrange("(p c) -> p c", p=P), rcount_r).then_inc(s["rcount_out"], 16)
            sp.wait_ge(s["rcount_out"], 16)
            sp.dma_start(rcount_l, rcount_d.rearrange("(b t p) -> t b p", b=2, p=P))\
                .then_inc(s["rcount_in"], 16)
            sp.wait_ge(s["setup_c"], 5)
            sp.dma_start(bias_d.rearrange("(a k) f -> a k f", a=1),
                         bias_part[:, :, :, :].rearrange("a k b f -> a (k b) f")).then_inc(s["bias_out"], 16)
            sp.wait_ge(s["bias_out"], 16)
            sp.dma_start(bias3[:, :, :], bias_d.rearrange("(k b) f -> k b f", b=2)).then_inc(s["bias_in"], 16)
            sp.wait_ge(s["masks_out"], 32)

            def edge_load(g, k, _=None):
                if not isinstance(g, int) or g < EG - 1:
                    wait(sp, s["a_T"], g - 3)
                    stand(sp, "gate_sp")
                    sp.dma_start(attr_sb[:, k, :, :],
                                 attr[bass.ds(g * GROUP, GROUP), :].rearrange("(j p) f -> p j f", p=P))\
                        .then_inc(attr_in[k], 16)
                if inside(g, EG):
                    wait(sp, s["a_scan"], g - 3)
                    stand(sp, "gate_sp")
                    sp.dma_start(same_sb[:, k, :],
                                 same_d[bass.ds(g * GROUP, GROUP)].unsqueeze(0).to_broadcast((P, GROUP)))\
                        .then_inc(same_in[k], 16)

            steps(sp, EG, 0, edge_load)

            sp.wait_ge(s["a_scan"], EG)

            def reset_load(g, k, _=None):
                if inside(g, EG):
                    wait(sp, s["e_keep"], g - 3)
                    stand(sp, "gate_sp")
                    sp.dma_start(reset_sb[:, k, :],
                                 reset_d[bass.ds(g * GROUP, GROUP)].unsqueeze(0).to_broadcast((P, GROUP)))\
                        .then_inc(reset_in[k], 16)

            for g in range(4):
                reset_load(g, g)

            sp.wait_ge(s["needs_made"], 1)

            def node_io(g, k, _=None):
                if inside(g, NG):
                    need = sp.value_load(need_scattered[:, bass.ds(g, 1)], min_val=1, max_val=EG)
                    wait(sp, s["n_T"], g - 3)
                    wait(sp, s["n_z"], g - 3)
                    stand(sp, "gate_sp")
                    sp.dma_start(xn[:, k, :, :], node_rows(x, g)).then_inc(node_in[k], 16)
                    sp.wait_ge(s["scattered"], need)
                    stand(sp, "gate_sp")
                    sp.dma_start(an[:, k, :, :], node_rows(table_d, g)).then_inc(node_in[k], 16)
                h, m = g - 5, (k - 5) % 4
                if inside(h, NG):
                    sp.wait_ge(s["n_x1"], h + 1)
                    if isinstance(h, int) and h == NG - 2:
                        sp.wait_ge(s["n_T"], NG)
                    if isinstance(h, int) and h == NG - 1:
                        sp.wait_ge(x1_out[(m - 1) % 4], slot_count(h - 1, (m - 1) % 4, 16))
                    stand(sp, "gate_sp")
                    sp.dma_start(node_rows(table_d, h), x1[:, m, :, :]).then_inc(x1_out[m], 16)
                h, m = g - 7, (k - 7) % 4
                if inside(h, NG):
                    sp.wait_ge(x1_out[m], slot_count(h, m, 16))
                    sp.sem_inc(s["stored"], 1)
                h, m = g - 8, k
                if inside(h, NG):
                    sp.wait_ge(s["n_out"], h + 1)
                    if isinstance(h, int) and h == NG - 1:
                        sp.wait_ge(o2_out[(m - 1) % 4], slot_count(h - 1, (m - 1) % 4, 16))
                    stand(sp, "gate_sp")
                    sp.dma_start(node_rows(out, h), o2[:, m, :, :]).then_inc(o2_out[m], 16)

            steps(sp, NG, 8, node_io)
            steps(sp, EG, 0, reset_load, begin=4)

        @block.gpsimd
        def _(pool):
            nc.gpsimd.iota(edge_no_i, pattern=[[1, EROW]], base=0, channel_multiplier=EROW)\
                .then_inc(s["iota_done"], 1)
            nc.gpsimd.iota(edge_end_i, pattern=[[0, 1]], base=GROUP, channel_multiplier=GROUP)\
                .then_inc(s["iota_done"], 1)
            nc.gpsimd.iota(base_i, pattern=[[GROUP, NG]], base=0, channel_multiplier=0).then_inc(s["iota_done"], 1)
            nc.gpsimd.iota(zbase_i, pattern=[[ZSTEP, EG]], base=0, channel_multiplier=0).then_inc(s["iota_done"], 1)

            def scatter(target, index, source, done):
                for j in range(TILES):
                    pool.indirect_dma_start(
                        out=target, out_offset=bass.IndirectOffsetOnAxis(ap=index[:, j:j + 1], axis=0),
                        in_=source(j), in_offset=None, bounds_check=NODES - 1, oob_is_err=False,
                    ).then_inc(done, 16)

            def gather(source, index, target, done):
                for j in range(TILES):
                    pool.indirect_dma_start(
                        out=target(j), out_offset=None, in_=source,
                        in_offset=bass.IndirectOffsetOnAxis(ap=index[:, j:j + 1], axis=0),
                        bounds_check=NODES - 1, oob_is_err=False,
                    ).then_inc(done, 16)

            pool.wait_ge(s["setup_v"], 20)
            pool.wait_ge(s["needs_made"], 1)

            for g in range(EG + 2):
                k, m = g % 4, (g - 2) % 4
                if g < EG:
                    pool.wait_ge(s["a_mean"], g + 1)
                    pool.wait_ge(s["zeroed"], pool.value_load(need_zeroed[:, g:g + 1], min_val=1, max_val=EG))
                    stand(pool, "gate")
                    scatter(table_d, scatter_i[:, g * TILES:(g + 1) * TILES], lambda j: rows[:, g, j, :], mean_out[k])
                if g >= 2:
                    pool.wait_ge(mean_out[m], slot_count(g - 2, m, 64))
                    pool.sem_inc(s["scattered"], 1)
            for g in range(EG):
                pool.wait_ge(s["stored"], pool.value_load(need_stored[:, g:g + 1], min_val=1, max_val=NG))
                wait(pool, dst_in[g % 4], slot_count(g, g % 4, 64, 1))
                stand(pool, "gate")
                gather(table_d, gather_i[:, g * TILES:(g + 1) * TILES], lambda j: rows[:, g, j, :], dst_in[g % 4])

            for semaphore, count in all_uses(x1_out, NG, 16):
                pool.wait_ge(semaphore, count)
            stand(pool, "gate")

            def layer1_rows(g, k, _=None):
                if inside(g, EG):
                    wait(pool, s["e_T"], g - 3)
                    wait(pool, gathered[k], slot_count(g, k, 64, 1))
                    stand(pool, "gate")
                    nc.gpsimd.tensor_copy(src_idx[:, k, :], src_i[:, bass.ds(g * TILES, TILES)])\
                        .then_inc(s["e_idx"], 1)
                    pool.wait_ge(s["e_idx"], g + 1)
                    stand(pool, "gate")
                    gather(table_d, src_idx[:, k, :], lambda j: xs[:, k, j, :], gathered[k])
                h = g - 12
                if inside(h, EG):
                    if isinstance(h, int) and h == 0:
                        for semaphore, count in all_uses(o2_out, NG, 16):
                            pool.wait_ge(semaphore, count)
                    wait(pool, o3_out[k], slot_count(h, k, 64, 1))
                    stand(pool, "gate")
                    nc.gpsimd.tensor_copy(out_idx[:, k, :], scatter_i[:, bass.ds(h * TILES, TILES)])\
                        .then_inc(s["e_idx2"], 1)
                    pool.wait_ge(s["e_idx2"], h + 1)
                    pool.wait_ge(s["e_out"], h + 1)
                    stand(pool, "gate")
                    scatter(out, out_idx[:, k, :], lambda j: o3[:, k, j, :], o3_out[k])

            steps(pool, EG, 12, layer1_rows)
            for semaphore, count in all_uses(o3_out, EG, 64):
                pool.wait_ge(semaphore, count)

        @block.scalar
        def _(act):
            act.wait_ge(s["zeros_set"], 1)

            def zero_fill(g, k, _=None):
                if inside(g, EG):
                    if isinstance(g, int) and g == EG - 1:
                        act.wait_ge(zero_out[(k - 1) % 4], slot_count(g - 1, (k - 1) % 4, 16))
                    base = min(g * ZSTEP, NODES - ZSTEP) if isinstance(g, int) else g * ZSTEP
                    act.dma_start(table_d[bass.ds(base, ZSTEP), :].rearrange("(p a b) f -> p a (b f)", p=P, b=4),
                                  zeros[:, :].unsqueeze(1).to_broadcast((P, ZROWS // 4, 4 * P)))\
                        .then_inc(zero_out[k], 16)
                h, m = g - 3, (k - 3) % 4
                if inside(h, EG):
                    act.wait_ge(zero_out[m], slot_count(h, m, 16))
                    act.sem_inc(s["zeroed"], 1)

            steps(act, EG, 3, zero_fill)

            def node_act(g, k, _=None):
                if inside(g, NG):
                    act.wait_ge(s["n_T"], g + 1)
                    wait(act, s["n_h"], g - 1)
                    nc.scalar.activation(xT[:, k % 2, :], banks[0][:, :], ACT.Copy)
                    nc.scalar.activation(aT[:, k % 2, :], banks[1][:, :], ACT.Copy).then_inc(s["n_evac"], 1)
                h, m = g - 1, (k - 1) % 4
                if inside(h, NG):
                    act.wait_ge(s["n_h"], h + 1)
                    wait(act, s["n_y"], h - 1)
                    for c in range(2):
                        i = nc.scalar.activation(hT[:, m % 2, c, :], banks[2 + 2 * (m % 2) + c][:, :], ACT.Relu,
                                                 bias=b1_sb[:, c:c + 1])
                    i.then_inc(s["n_relu"], 1)
                h, m = g - 3, (k - 3) % 4
                if inside(h, NG):
                    act.wait_ge(s["n_aggr"], h + 1)
                    nc.scalar.activation(sd1[:, m, :], mv1[:, m, :, 1], ACT.Sqrt, bias=eps[:, :])\
                        .then_inc(s["n_sd"], 1)
                h, m = g - 5, (k - 5) % 4
                if inside(h, NG):
                    act.wait_ge(s["n_aggr2"], h + 1)
                    nc.scalar.activation(sd2[:, m, :], mv2[:, m, :, 1], ACT.Sqrt, bias=eps[:, :])\
                        .then_inc(s["n_sd2"], 1)
                h, m = g - 6, (k - 6) % 4
                if inside(h, NG):
                    act.wait_ge(s["n_nb2"], h + 1)
                    for j in range(TILES):
                        i = nc.scalar.activation(o2[:, m, j, :], o2[:, m, j, :], ACT.Identity,
                                                 bias=nb2[:, m, j:j + 1], scale=rs2[:, m, j:j + 1])
                    i.then_inc(s["n_out"], 1)

            steps(act, NG, 6, node_act)

            act.wait_ge(s["n_x1"], NG)
            act.wait_ge(s["n_h"], NG)
            act.wait_ge(s["n_y"], NG)
            for semaphore, count in all_uses(o2_out, NG, 16):
                act.wait_ge(semaphore, count)

            def row_copy(h, m):
                if inside(h, EG):
                    act.wait_ge(dst_in[m], slot_count(h, m, 64))
                    wait(act, s["e_T"], h - 1)
                    nc.scalar.activation(xd[:, m % 2, :],
                                         rows[:, bass.ds(h, 1), :, :].rearrange("p g j f -> p (g j f)"), ACT.Copy)\
                        .then_inc(s["e_xd"], 1)

            row_copy(0, 0)

            def edge_act(g, k, q):
                h = g - 8
                four = 1 if isinstance(h, int) and h == EG - 1 else 4
                if k == 0 and inside(h, EG):
                    act.wait_ge(s["e_aggr"], h + four)
                    act.activation(sd3[:, 0:four, :], mv3[:, 0:four, :, 1], ACT.Sqrt, bias=eps[:, :])\
                        .then_inc(s["e_sd"], 1)
                if inside(g, EG):
                    act.wait_ge(s["e_T"], g + 1)
                    wait(act, s["e_v"], g - 1)
                    nc.scalar.activation(xsT[:, k % 2, :], banks[0][:, :], ACT.Copy)
                    nc.scalar.activation(xdT[:, k % 2, :], banks[1][:, :], ACT.Copy).then_inc(s["e_evac"], 1)
                h, m = g - 1, (k - 1) % 4
                if inside(h, EG):
                    act.wait_ge(s["e_q"], h + 1)
                    wait(act, s["e_qk"], h)
                    nc.scalar.activation(qT, banks[2][:, :], ACT.Identity, bias=qkvb_sb[:, 0:1])\
                        .then_inc(s["e_qT"], 1)
                    act.wait_ge(s["e_v"], h + 1)
                    wait(act, s["e_pv"], h - 1)
                    nc.scalar.activation(vT[:, m % 2, :], banks[2][:, :], ACT.Identity, bias=qkvb_sb[:, 2:3])\
                        .then_inc(s["e_vT"], 1)
                h = g - 4
                if inside(h, EG):
                    act.wait_ge(s["e_attnT"], h + 1)
                    wait(act, s["e_o"], h)
                    nc.scalar.activation(attnT, banks[6][:, :], ACT.Copy).then_inc(s["e_attnTs"], 1)
                h, m = g - 8, k
                if inside(h, EG):
                    act.wait_ge(s["e_nb"], q - 1)
                    wait(act, o3_out[m], slot_count(h, m, 64, 1))
                    for j in range(TILES):
                        i = nc.scalar.activation(o3[:, m, j, :], z3[:, m, j, :], ACT.Identity,
                                                 bias=nb3[:, m, j:j + 1], scale=rs3[:, m, j:j + 1])
                    i.then_inc(s["e_out"], 1)
                row_copy(g + 1, (k + 1) % 4)
                h = g - 2
                if inside(h, EG):
                    act.wait_ge(s["e_drop"], h + 1)
                    wait(act, s["e_acc"], h)
                    nc.scalar.activation(decay, drop, ACT.Exp).then_inc(s["e_decay"], 1)
                    act.wait_ge(s["e_rise"], h + 1)
                    nc.scalar.activation(prob[:, :], rise, ACT.Exp).then_inc(s["e_prob"], 1)

            steps(act, EG, 8, edge_act)

        @block.vector
        def _(dve):
            V = nc.vector
            done = [0, 0]

            def then(ins):
                done[0] += 1
                ins.then_inc(s["setup_v"], 1)
                dve.wait_ge(s["setup_v"], done[0])

            def thenc(ins):
                done[1] += 1
                ins.then_inc(s["setup_c"], 1)
                dve.wait_ge(s["setup_c"], done[1])

            V.memset(zeros[:, :], 0.0).then_inc(s["zeros_set"], 1)
            V.memset(attr_tail[:, :, :], 0.0).then_inc(s["zeros_set"], 1)
            V.memset(ones3[:, :], 1.0)
            V.memset(one1[:, :], 1.0)
            V.memset(start_row[:, :], 0.0)
            V.memset(mx[:, 0, 0:1], -FAR)
            V.memset(eps[:, :], EPS).then_inc(s["consts_set"], 1)
            dve.wait_ge(s["rows_in"], 32)
            dve.wait_ge(s["iota_done"], 4)
            dve.wait_ge(s["consts_set"], 1)
            then(V.tensor_copy(cur_rf, cur_r))
            then(V.tensor_copy(prev_rf, prev_r))
            then(V.tensor_tensor(same_r, cur_rf, prev_rf, ALU.is_equal))
            then(V.tensor_copy(same_bf[:, :], same_r))
            then(V.tensor_scalar(reset_bf[:, :], same_r, 2.0 * FAR, -FAR, ALU.mult, ALU.add))
            then(V.tensor_copy(edge_no, edge_no_i))
            then(V.tensor_tensor(first_r, edge_no, same_r, ALU.mult))
            then(V.tensor_tensor(first_r, edge_no, first_r, ALU.subtract))
            then(V.tensor_tensor_scan(start_r, first_r, first_r, 0.0, ALU.max, ALU.max))
            dve.wait_ge(s["setup_t"], 1)
            then(V.tensor_tensor_scan(start_row[:, 1:P + 1], banks[7][0:1, 0:P], start_row[:, 0:1].to_broadcast((1, P)),
                                      0.0, ALU.max, ALU.max))
            dve.wait_ge(s["setup_t"], 2)
            then(V.tensor_copy(start_in[:, :], banks[6][:, 0:1]))
            then(V.tensor_scalar(count_r, start_r, start_in[:, :], None, ALU.max))
            then(V.scalar_tensor_tensor(count_r, edge_no, 1.0, count_r, ALU.add, ALU.subtract))
            then(V.reciprocal(rcount_r, count_r))
            dve.wait_ge(s["tiles_in"], 48)
            then(V.tensor_copy(dst_f, dst_i))
            then(V.tensor_copy(next_f, next_i))
            then(V.tensor_tensor(inner_f, dst_f, next_f, ALU.is_equal))
            then(V.scalar_tensor_tensor(scatter_f, inner_f, SKIP, dst_f, ALU.mult, ALU.add))
            then(V.tensor_copy(scatter_i[:, :], scatter_f))
            then(V.tensor_scalar(gather_i[:, :], dst_f, float(NODES - 1), None, ALU.min))
            dve.wait_ge(s["needs_in"], 32)
            then(V.memset(needs[:, :], 1.0))
            then(V.tensor_copy(first_f, first_i))
            then(V.tensor_copy(edge_end, edge_end_i))
            then(V.tensor_scalar(last_f, last_i, float(NODES - 1), None, ALU.min))
            then(V.tensor_scalar(base_f, base_i, float(NODES - GROUP), None, ALU.min))
            then(V.tensor_scalar(zbase_f, zbase_i, float(NODES - ZSTEP), None, ALU.min))
            then(V.tensor_scalar(first_c, first_f, edge_end[0:NG, :], None, ALU.is_lt, ALU.add,
                                 accum_out=needs[0:NG, 0:1]))
            then(V.tensor_scalar(base_c, base_f, last_f, None, ALU.is_le, ALU.add, accum_out=needs[0:EG, 1:2]))
            then(V.tensor_scalar(zbase_c, zbase_f, last_f, None, ALU.is_le, ALU.add, accum_out=needs[0:EG, 2:3]))
            dve.wait_ge(s["setup_t"], 3)
            V.tensor_scalar(needs_i[:, :], banks[5][0:1, 0:3 * P], 1.0, None, ALU.max).then_inc(s["needs_made"], 1)
            dve.wait_ge(s["weights_in"], 16 * 11)
            thenc(V.tensor_copy(bias_part[:, 0, :, :], bias_row[:, :, :]))
            thenc(V.tensor_tensor(bias_left[:, 0, :, :], bias_row[:, :, :], bias_part[:, 0, :, :], ALU.subtract))
            thenc(V.tensor_copy(bias_part[:, 1, :, :], bias_left[:, 0, :, :]))
            thenc(V.tensor_tensor(bias_left[:, 1, :, :], bias_left[:, 0, :, :], bias_part[:, 1, :, :], ALU.subtract))
            thenc(V.tensor_copy(bias_part[:, 2, :, :], bias_left[:, 1, :, :]))
            dve.wait_ge(s["setup_t"], 5)
            for b in range(2):
                V.tensor_copy(rcount_t[:, b * (ET // 2):(b + 1) * (ET // 2)], banks[4 + b][:, 0:ET // 2])\
                    .then_inc(s["setup_c"], 1)

            def sums(g, k, _=None):
                if inside(g, EG):
                    dve.wait_ge(s["a_T"], g + 1)
                    dve.wait_ge(same_in[k], slot_count(g, k, 16))
                    wait(dve, s["a_back"], g - 3)
                    wait(dve, s["a_scan"], g)
                    start = 0.0 if isinstance(g, int) and g == 0 else sumT[:, (k - 1) % 4, GROUP - 1:GROUP]
                    V.tensor_tensor_scan(sumT[:, k, :], same_sb[:, k, :], banks[k % 2][:, :], start,
                                         ALU.mult, ALU.add).then_inc(s["a_scan"], 1)
                h, m = g - 1, (k - 1) % 4
                if inside(h, EG):
                    dve.wait_ge(s["a_back"], h + 1)
                    for j in range(TILES):
                        i = V.tensor_scalar(rows[:, bass.ds(h, 1), j, :].rearrange("p g f -> p (g f)"),
                                            banks[2 + m % 2][:, j * P:(j + 1) * P],
                                            rcount_t[:, bass.ds(h * TILES + j, 1)], None, ALU.mult)
                    i.then_inc(s["a_mean"], 1)

            steps(dve, EG, 1, sums)

            def norm_stats(z, stats, mv, stats_done, mv_done, h):
                for j in range(TILES):
                    i = V.bn_stats(stats[:, j, :], z[:, j, :])
                i.then_inc(stats_done, 1)
                dve.wait_ge(stats_done, h + 1)
                stand(dve, "gate_dve")
                for j in range(TILES):
                    i = V.bn_aggr(mv[:, j, :], stats[:, j, :])
                i.then_inc(mv_done, 1)

            def node_dve(g, k, _=None):
                h, m = g - 2, (k - 2) % 4
                if inside(h, NG):
                    dve.wait_ge(s["n_y"], h + 1)
                    wait(dve, x1_out[m], slot_count(h, m, 16, 1))
                    V.tensor_tensor(x1[:, m, :, :].rearrange("p j f -> p (j f)"), banks[6 + m % 2][:, :],
                                    xn[:, m, :, :].rearrange("p j f -> p (j f)"), ALU.add).then_inc(s["n_z"], 1)
                    dve.wait_ge(s["n_z"], h + 1)
                    norm_stats(x1[:, m], st1[:, m % 2], mv1[:, m], s["n_stats"], s["n_aggr"], h)
                h, m = g - 3, (k - 3) % 4
                if inside(h, NG):
                    dve.wait_ge(s["n_sd"], h + 1)
                    V.reciprocal(rs1[:, m, :], sd1[:, m, :]).then_inc(s["n_rs"], 1)
                    dve.wait_ge(s["n_rs"], h + 1)
                    for j in range(TILES):
                        i = V.tensor_scalar(x1[:, m, j, :], x1[:, m, j, :], mv1[:, m, j, 0:1], rs1[:, m, j:j + 1],
                                            ALU.subtract, ALU.mult)
                    i.then_inc(s["n_x1"], 1)
                h, m = g - 4, (k - 4) % 4
                if inside(h, NG):
                    dve.wait_ge(s["n_x1"], h + 1)
                    wait(dve, o2_out[m], slot_count(h, m, 16, 1))
                    V.tensor_tensor(o2[:, m, :, :], x1[:, m, :, :],
                                    outb_bc[:, :].unsqueeze(1).to_broadcast((P, TILES, P)), ALU.add)\
                        .then_inc(s["n_z2"], 1)
                    dve.wait_ge(s["n_z2"], h + 1)
                    norm_stats(o2[:, m], st2[:, m % 2], mv2[:, m], s["n_stats2"], s["n_aggr2"], h)
                h, m = g - 5, (k - 5) % 4
                if inside(h, NG):
                    dve.wait_ge(s["n_sd2"], h + 1)
                    V.reciprocal(rs2[:, m, :], sd2[:, m, :]).then_inc(s["n_rs2"], 1)
                    dve.wait_ge(s["n_rs2"], h + 1)
                    V.scalar_tensor_tensor(nb2[:, m, :], mv2[:, m, :, 0], -1.0, rs2[:, m, :], ALU.mult, ALU.mult)\
                        .then_inc(s["n_nb2"], 1)

            steps(dve, NG, 5, node_dve)

            def edge_dve(g, k, q):
                h = g - 8
                if k == 0 and inside(h, EG):
                    n = 1 if isinstance(h, int) and h == EG - 1 else 4
                    dve.wait_ge(s["e_sd"], q - 1)
                    wait(dve, s["e_out"], h)
                    V.reciprocal(rs3[:, 0:n, :], sd3[:, 0:n, :]).then_inc(s["e_rs"], 1)
                    dve.wait_ge(s["e_rs"], q - 1)
                    V.scalar_tensor_tensor(nb3[:, 0:n, :], mv3[:, 0:n, :, 0], -1.0, rs3[:, 0:n, :],
                                           ALU.mult, ALU.mult).then_inc(s["e_nb"], 1)
                h = g - 4
                if inside(h, EG):
                    dve.wait_ge(s["e_back"], h + 1)
                    V.reciprocal(rden[:, :, :].rearrange("p j h -> p (j h)"), banks[4][:, 0:GROUP:HD])\
                        .then_inc(s["e_rden"], 1)
                    dve.wait_ge(s["e_rden"], h + 1)
                    wait(dve, s["e_attnT"], h)
                    V.tensor_tensor(attn[:, :, :].rearrange("p j (h d) -> p (j h) d", d=HD),
                                    banks[6][:, :].rearrange("p (a d) -> p a d", d=HD),
                                    rden[:, :, :].rearrange("p j h -> p (j h)").unsqueeze(2)
                                    .to_broadcast((P, TILES * HEADS, HD)), ALU.mult).then_inc(s["e_attn"], 1)
                h, m = g - 1, (k - 1) % 4
                if inside(h, EG):
                    dve.wait_ge(s["e_qT"], h + 1)
                    dve.wait_ge(s["e_k"], h + 1)
                    wait(dve, s["e_s"], h - 1)
                    V.scalar_tensor_tensor(qk[:, m % 2, :], banks[3][:, :], qkvb_sb[:, 1:2], qT, ALU.add, ALU.mult)\
                        .then_inc(s["e_qk"], 1)
                h, m = g - 2, (k - 2) % 4
                if inside(h, EG):
                    dve.wait_ge(s["e_s"], h + 1)
                    dve.wait_ge(reset_in[m], slot_count(h, m, 16))
                    wait(dve, s["e_carry"], h)
                    V.tensor_tensor_scan(mx[:, m, 1:GROUP + 1], reset_sb[:, m, :], banks[5][:, :],
                                         mx[:, m, 0:1], ALU.min, ALU.max).then_inc(s["e_mx"], 1)
                    dve.wait_ge(s["e_mx"], h + 1)
                    V.tensor_copy(mx[:, (m + 1) % 4, 0:1], mx[:, m, GROUP:GROUP + 1]).then_inc(s["e_carry"], 1)
                    V.tensor_tensor(keep, mx[:, m, 0:GROUP], reset_sb[:, m, :], ALU.min)\
                        .then_inc(s["e_keep"], 1)
                    dve.wait_ge(s["e_keep"], h + 1)
                    wait(dve, s["e_decay"], h)
                    V.tensor_tensor(drop, keep, mx[:, m, 1:GROUP + 1], ALU.subtract)\
                        .then_inc(s["e_drop"], 1)
                    wait(dve, s["e_prob"], h)
                    V.tensor_tensor(rise, banks[5][:, :], mx[:, m, 1:GROUP + 1], ALU.subtract)\
                        .then_inc(s["e_rise"], 1)
                h, m = g - 4, k
                if inside(h, EG):
                    dve.wait_ge(s["e_o"], h + 1)
                    wait(dve, s["e_out"], h - 3)
                    V.tensor_tensor(z3[:, m, :, :].rearrange("p j f -> p (j f)"), banks[7][:, :],
                                    rows[:, bass.ds(h, 1), :, :].rearrange("p g j f -> p (g j f)"), ALU.add)\
                        .then_inc(s["e_z"], 1)
                    dve.wait_ge(s["e_z"], h + 1)
                    norm_stats(z3[:, m], st3, mv3[:, m], s["e_stats"], s["e_aggr"], h)
                h, m = g - 2, (k - 2) % 4
                if inside(h, EG):
                    first = isinstance(h, int) and h == 0
                    dve.wait_ge(s["e_prob"], h + 1)
                    dve.wait_ge(s["e_vT"], h + 1)
                    V.tensor_tensor(pv[:, :], vT[:, m % 2, :], prob[:, :], ALU.mult).then_inc(s["e_pv"], 1)
                    dve.wait_ge(s["e_decay"], h + 1)
                    wait(dve, s["e_den"], h)
                    wait(dve, s["e_back"], h - 1)
                    V.tensor_tensor_scan(den[:, m % 2, :], decay, prob[:, :],
                                         0.0 if first else den[:, (m + 1) % 2, GROUP - 1:GROUP],
                                         ALU.mult, ALU.add).then_inc(s["e_den"], 1)
                    dve.wait_ge(s["e_pv"], h + 1)
                    wait(dve, s["e_acc"], h)
                    V.tensor_tensor_scan(acc[:, m % 2, :], decay, pv[:, :],
                                         0.0 if first else acc[:, (m + 1) % 2, GROUP - 1:GROUP],
                                         ALU.mult, ALU.add).then_inc(s["e_acc"], 1)

            steps(dve, EG, 8, edge_dve)

        @block.tensor
        def _(pe):
            T = nc.tensor
            pe.wait_ge(s["weights_in"], 16 * 11)
            pe.wait_ge(s["consts_set"], 1)
            pe.wait_ge(s["setup_v"], 9)
            T.transpose(banks[7][0:1, 0:P], start_r[:, EROW - 1:EROW], ident[:, :]).then_inc(s["setup_t"], 1)
            pe.wait_ge(s["setup_v"], 10)
            T.matmul(banks[6][:, 0:1], start_row[:, 0:P], one1[:, :], start=True, stop=True)\
                .then_inc(s["setup_t"], 1)
            pe.wait_ge(s["setup_v"], 29)
            for c in range(3):
                i = T.transpose(banks[5][0:1, c * P:(c + 1) * P], needs[:, c:c + 1], ident[:, :])
            i.then_inc(s["setup_t"], 1)
            pe.wait_ge(s["needs_made"], 1)
            pe.wait_ge(s["rcount_in"], 16)
            for b in range(2):
                T.transpose(banks[4 + b][:, 0:ET // 2], rcount_l[:, b, :], ident[0:ET // 2, 0:ET // 2])\
                    .then_inc(s["setup_t"], 1)
            pe.wait_ge(s["attr_tail_in"], 32)

            def edge_sums(g, k, _=None):
                if inside(g, EG):
                    last = isinstance(g, int) and g == EG - 1
                    if not last:
                        pe.wait_ge(attr_in[k], slot_count(g, k, 16))
                    wait(pe, s["a_scan"], g - 1)
                    for j in range(TILES):
                        src = attr_tail[:, j, :] if last else attr_sb[:, k, j, :]
                        i = T.transpose(banks[k % 2][:, j * P:(j + 1) * P], src, ident[:, :])
                    i.then_inc(s["a_T"], 1)
                h, m = g - 1, (k - 1) % 4
                if inside(h, EG):
                    pe.wait_ge(s["a_scan"], h + 1)
                    wait(pe, s["a_mean"], h - 1)
                    for j in range(TILES):
                        i = T.transpose(banks[2 + m % 2][:, j * P:(j + 1) * P], sumT[:, m, j * P:(j + 1) * P],
                                        ident[:, :])
                    i.then_inc(s["a_back"], 1)

            steps(pe, EG, 1, edge_sums)
            pe.wait_ge(s["a_mean"], EG)
            pe.wait_ge(s["setup_c"], 7)
            pe.wait_ge(s["bias_in"], 16)

            def node_pe(g, k, _=None):
                if inside(g, NG):
                    pe.wait_ge(node_in[k], slot_count(g, k, 32))
                    wait(pe, s["n_evac"], g)
                    for src, bank in ((xn, 0), (an, 1)):
                        for j in range(TILES):
                            i = T.transpose(banks[bank][:, j * P:(j + 1) * P], src[:, k, j, :], ident[:, :])
                    i.then_inc(s["n_T"], 1)
                h, m = g - 1, (k - 1) % 4
                if inside(h, NG):
                    pe.wait_ge(s["n_evac"], h + 1)
                    wait(pe, s["n_relu"], h - 1)
                    for c in range(2):
                        bank = banks[2 + 2 * (m % 2) + c]
                        T.matmul(bank[:, :], w1_sb[:, 0, c * P:(c + 1) * P], xT[:, m % 2, :], start=True, stop=False)
                        i = T.matmul(bank[:, :], w1_sb[:, 1, c * P:(c + 1) * P], aT[:, m % 2, :],
                                     start=False, stop=True)
                    i.then_inc(s["n_h"], 1)
                h, m = g - 2, (k - 2) % 4
                if inside(h, NG):
                    pe.wait_ge(s["n_relu"], h + 1)
                    wait(pe, s["n_z"], h - 1)
                    bank = banks[6 + m % 2]
                    T.matmul(bank[:, :], ones3[:, :], bias3[:, 0, :].unsqueeze(1).to_broadcast((3, TILES, P)),
                             start=True, stop=False)
                    for j in range(TILES):
                        for c in range(2):
                            i = T.matmul(bank[:, j * P:(j + 1) * P], hT[:, m % 2, c, j * P:(j + 1) * P],
                                         w2_sb[:, c, :], start=False, stop=(c == 1 and j == TILES - 1))
                    i.then_inc(s["n_y"], 1)

            steps(pe, NG, 2, node_pe)
            pe.wait_ge(s["n_z"], NG)
            pe.wait_ge(s["n_relu"], NG)

            def edge_pe(g, k, _=None):
                if inside(g, EG):
                    pe.wait_ge(gathered[k], slot_count(g, k, 64))
                    wait(pe, s["e_evac"], g)
                    for j in range(TILES):
                        T.transpose(banks[0][:, j * P:(j + 1) * P], xs[:, k, j, :], ident[:, :])
                    pe.wait_ge(s["e_xd"], g + 1)
                    for j in range(TILES):
                        i = T.transpose(banks[1][:, j * P:(j + 1) * P], xd[:, k % 2, j * P:(j + 1) * P], ident[:, :])
                    i.then_inc(s["e_T"], 1)
                h, m = g - 1, (k - 1) % 4
                if inside(h, EG):
                    pe.wait_ge(s["e_evac"], h + 1)
                    wait(pe, s["e_vT"], h)
                    T.matmul(banks[2][:, :], qkvw_sb[:, 0:P], xdT[:, m % 2, :], start=True, stop=True)\
                        .then_inc(s["e_q"], 1)
                    wait(pe, s["e_qk"], h)
                    T.matmul(banks[3][:, :], qkvw_sb[:, P:2 * P], xsT[:, m % 2, :], start=True, stop=True)\
                        .then_inc(s["e_k"], 1)
                    pe.wait_ge(s["e_qT"], h + 1)
                    T.matmul(banks[2][:, :], qkvw_sb[:, 2 * P:3 * P], xsT[:, m % 2, :], start=True, stop=True)\
                        .then_inc(s["e_v"], 1)
                h, m = g - 2, (k - 2) % 4
                if inside(h, EG):
                    pe.wait_ge(s["e_qk"], h + 1)
                    wait(pe, s["e_rise"], h)
                    T.matmul(banks[5][:, :], head_sum[:, :], qk[:, m % 2, :], start=True, stop=True)\
                        .then_inc(s["e_s"], 1)
                h, m = g - 4, k
                if inside(h, EG):
                    pe.wait_ge(s["e_attn"], h + 1)
                    for j in range(TILES):
                        i = T.transpose(banks[6][:, j * P:(j + 1) * P], attn[:, j, :], ident[:, :])
                    i.then_inc(s["e_attnT"], 1)
                h, m = g - 4, k
                if inside(h, EG):
                    pe.wait_ge(s["e_attnTs"], h + 1)
                    wait(pe, s["e_z"], h)
                    T.matmul(banks[7][:, :], ones3[:, :], bias3[:, 1, :].unsqueeze(1).to_broadcast((3, TILES, P)),
                             start=True, stop=False)
                    for j in range(TILES):
                        i = T.matmul(banks[7][:, j * P:(j + 1) * P], attnT[:, j * P:(j + 1) * P], outw_sb[:, :],
                                     start=False, stop=(j == TILES - 1))
                    i.then_inc(s["e_o"], 1)
                h, m = g - 3, (k - 3) % 4
                if inside(h, EG):
                    pe.wait_ge(s["e_acc"], h + 1)
                    wait(pe, s["e_attnTs"], h)
                    wait(pe, s["e_rden"], h)
                    for j in range(TILES):
                        T.transpose(banks[6][:, j * P:(j + 1) * P], acc[:, m % 2, j * P:(j + 1) * P], ident[:, :])
                    for j in range(TILES):
                        i = T.transpose(banks[4][:, j * P:(j + 1) * P], den[:, m % 2, j * P:(j + 1) * P], ident[:, :])
                    i.then_inc(s["e_back"], 1)

            steps(pe, EG, 4, edge_pe)


def kernel(x, src, dst, edge_attr_128, L0_gnn_W1, L0_gnn_b1, L0_gnn_W2, L0_gnn_b2, L1_gnn_qkv_w, L1_gnn_qkv_b,
           L1_gnn_out_w, L1_gnn_out_b):
    import numpy as np
    import concourse.bacc as bacc
    from concourse.bass_utils import run_bass_kernel_spmd as run

    src, dst = np.asarray(src), np.asarray(dst)
    pad = EPAD - EDGES
    dst_p = np.concatenate([dst, np.full(pad, PAD_NODE, dst.dtype)])
    next_p = np.concatenate([dst[1:], np.full(pad + 1, PAD_NODE, dst.dtype)])
    prev_p = np.concatenate([np.full(1, -1, dst.dtype), dst_p[:-1]])
    src_p = np.concatenate([src, np.zeros(pad, src.dtype)])
    head = np.arange(P) // HD
    ins = {
        "x": x, "attr": edge_attr_128,
        "dst_tile": dst_p.reshape(ET, P).T, "next_tile": next_p.reshape(ET, P).T, "src_tile": src_p.reshape(ET, P).T,
        "first_dst": dst_p[::GROUP].reshape(1, EG), "last_dst": dst_p[GROUP - 1::GROUP].reshape(EG, 1),
        "dst_row": dst_p.reshape(P, EROW), "prev_row": prev_p.reshape(P, EROW),
        "w1": L0_gnn_W1, "b1": np.asarray(L0_gnn_b1).reshape(2, P).T,
        "w2": L0_gnn_W2, "b2": np.asarray(L0_gnn_b2).reshape(1, P),
        "qkv_wT": np.asarray(L1_gnn_qkv_w).T, "qkv_b": np.asarray(L1_gnn_qkv_b).reshape(3, P).T,
        "out_wT": np.asarray(L1_gnn_out_w).T, "out_b": np.asarray(L1_gnn_out_b).reshape(1, P),
        "ident_c": np.eye(P, dtype=np.float32),
        "head_sum_c": (head[:, None] == head[None, :]).astype(np.float32) * np.float32(HD ** -0.5),
    }
    ins = {k: np.ascontiguousarray(v) for k, v in ins.items()}
    nc = bacc.Bacc("TRN2", target_bir_lowering=False, num_devices=1)
    args = {k: nc.dram_tensor(k, v.shape, mybir.dt.from_np(v.dtype), kind="ExternalInput").ap()
            for k, v in ins.items()}
    out = nc.dram_tensor("out", (NODES, P), F32, kind="ExternalOutput").ap()
    build(nc, out=out, **args)
    r = run(nc, [ins], core_ids=[0])
    return r.results[0]["out"]
```

```python
from contextlib import ExitStack

import concourse.bass as bass
from concourse import mybir

F32 = mybir.dt.float32
BF16 = mybir.dt.bfloat16
F32R = mybir.dt.float32r
I32 = mybir.dt.int32
ALU = mybir.AluOpType
ACT = mybir.ActivationFunctionType

P = 128
NODES = 50000
EDGES = 25000
TILES = 4
GROUP = TILES * P
NG = -(-NODES // GROUP)
EG = -(-EDGES // GROUP)
EPAD = EG * GROUP
ET = EPAD // P
EROW = EPAD // P
HID = 256
HEADS = 8
HD = P // HEADS
EPS = 1e-5
FAR = 1.0e30
PAD_NODE = NODES
SKIP = 65536.0
ZROWS = -(-NODES // (EG * P))
ZSTEP = P * ZROWS
ZFILLS = 3
ZFIRST = EG - 1 - EG // 4 * ZFILLS
SINGLE = (EG - 1) // 4 * 4 - 4
UNROLL = 8
NORM1_DVE = 1
LATE = 1


def build(nc, x, attr, dst_tile, next_tile, src_tile, dst_row, prev_row, first_dst, last_dst, w1, b1, w2, b2, qkv_wT, qkv_b, out_wT,
          out_b, ident_c, head_sum_c, out):
    table_d = nc.dram_tensor("table_scratch", (NODES, P), F32).ap()
    same_d = nc.dram_tensor("same_scratch", (EPAD,), BF16).ap()
    reset_d = nc.dram_tensor("reset_scratch", (EPAD,), BF16).ap()
    rcount_d = nc.dram_tensor("rcount_scratch", (EPAD,), F32).ap()
    bias_d = nc.dram_tensor("bias_scratch", (6, P), BF16).ap()

    ctx = ExitStack()
    with ctx:
        def sb(name, shape, dt=F32):
            return ctx.enter_context(nc.sbuf_tensor(name, shape, dt))

        def sem(name):
            return ctx.enter_context(nc.semaphore(name))

        ident = sb("ident", [P, P])
        head_sum = sb("head_sum", [P, P])
        prob, pv = sb("prob", [P, GROUP]), sb("pv", [P, GROUP])
        w1_sb = prob[:, :].rearrange("p (c h) -> p c h", h=HID)
        w2_sb = sb("w2_sb", [P, 2, P])
        qkvw_sb = sb("qkvw_sb", [P, 3 * P])
        outw_sb = sb("outw_sb", [P, P])
        b1_sb = sb("b1_sb", [P, 2])
        qkvb_sb = sb("qkvb_sb", [P, 3])
        outb_bc = sb("outb_bc", [P, P])
        bias_row = sb("bias_row", [1, 2, P])
        bias_left = sb("bias_left", [1, 2, 2, P])
        bias_part = sb("bias_part", [1, 3, 2, P], BF16)
        bias3 = sb("bias3", [3, 2, P], BF16)
        ones3 = sb("ones3", [3, P], BF16)
        one1 = sb("one1", [1, 1])
        eps = sb("eps", [P, 1])
        zeros = sb("zeros", [P, 4 * P])

        src_i = sb("src_i", [P, ET], I32)
        scatter_i = sb("scatter_i", [P, ET], I32)
        gather_i = sb("gather_i", [P, ET], I32)
        rcount_t = sb("rcount_t", [P, ET])
        start_row = sb("start_row", [1, P + 1])
        start_in = sb("start_in", [P, 1])
        needs = sb("needs", [P, 3])
        needs_i = sb("needs_i", [1, 3 * P], I32)
        need_scattered = needs_i[:, 0:NG]
        need_stored = needs_i[:, P:P + EG]
        need_zeroed = needs_i[:, 2 * P:2 * P + EG]

        w1_hi, w1_lo = sb("w1_hi", [P, 2, HID], F32R), sb("w1_lo", [P, 2, HID], F32R)
        with ExitStack() as lent:
            x_hi, x_lo, a_hi, a_lo = (lent.enter_context(nc.sbuf_tensor(n, [P, 2, GROUP], F32R))
                                      for n in ("x_hi", "x_lo", "a_hi", "a_lo"))
        attr_sb = sb("attr_sb", [P, 4, TILES, P])
        sumT = sb("sumT", [P, 4, GROUP])

        rows = sb("rows", [P, EG, TILES, P])
        attr_tail = sb("attr_tail", [P, TILES, P])
        reset_sb = sb("reset_sb", [P, 4, GROUP], BF16)

        xn = sb("xn", [P, 4, TILES, P])
        an = sb("an", [P, 4, TILES, P])
        xT = sb("xT", [P, 2, GROUP])
        aT = sb("aT", [P, 2, GROUP])
        hT = sb("hT", [P, 2, 2, GROUP])
        x1 = sb("x1", [P, 4, TILES, P])
        o2 = sb("o2", [P, 4, TILES, P])
        st1 = sb("st1", [P, 2, TILES, 6])
        mv1 = sb("mv1", [P, 4, TILES, 2])
        sd1 = sb("sd1", [P, 4, TILES])
        rs1 = sb("rs1", [P, 4, TILES])
        nb1 = sb("nb1", [P, 4, TILES])
        st2 = sb("st2", [P, 2, TILES, 6])
        mv2 = sb("mv2", [P, 4, TILES, 2])
        sd2 = sb("sd2", [P, 4, TILES])
        rs2 = sb("rs2", [P, 4, TILES])
        nb2 = sb("nb2", [P, 4, TILES])

        def lend(tensor, n, cols, dt=F32, parts=P):
            flat = tensor[:, :, :, :].rearrange("p a b c -> p (a b c)")[0:parts, n * EROW:n * EROW + cols]
            return flat if dt == F32 else flat.bitcast(dt)

        cur_r, prev_r = lend(hT, 0, EROW, I32), lend(hT, 1, EROW, I32)
        cur_rf, prev_rf, same_r = (lend(hT, n, EROW) for n in (2, 3, 4))
        edge_no_i = lend(hT, 5, EROW, I32)
        edge_no, first_r, start_r, count_r = (lend(hT, n, EROW) for n in (6, 7, 8, 9))
        rcount_r = lend(x1, 0, EROW)
        dst_i, next_i = lend(x1, 1, EROW, I32), lend(x1, 2, EROW, I32)
        dst_f, next_f, inner_f, scatter_f = (lend(x1, n, EROW) for n in (3, 4, 5, 6))
        first_i, first_f, first_c = lend(x1, 7, EG, I32, NG), lend(x1, 8, EG, parts=NG), lend(x1, 9, EG, parts=NG)
        edge_end_i, edge_end = lend(o2, 0, 1, I32), lend(o2, 1, 1)
        last_i, last_f = lend(o2, 2, 1, I32, EG), lend(o2, 3, 1, parts=EG)
        base_i, base_f, base_c = lend(o2, 4, NG, I32, EG), lend(o2, 5, NG, parts=EG), lend(o2, 6, NG, parts=EG)
        zbase_i, zbase_f, zbase_c = lend(o2, 7, EG, I32, EG), lend(o2, 8, EG, parts=EG), lend(o2, 9, EG, parts=EG)
        same_bf = sb("same_bf", [P, EROW], BF16)
        reset_bf = sb("reset_bf", [P, EROW], BF16)
        rcount_l = xn[0:ET // 2, 0, 0:2, :]
        same_sb = an[:, 3, :, :].rearrange("p j f -> p (j f)").bitcast(BF16).rearrange("p (a e) -> p a e", e=GROUP)

        src_idx = sb("src_idx", [P, 4, TILES], I32)
        out_idx = sb("out_idx", [P, 4, TILES], I32)
        xs = attr_sb
        xsT, xdT = xT, aT
        qT, keep = hT[:, 0, 0, :], hT[:, 0, 1, :]
        qk = hT[:, 1, :, :]
        vT = o2[:, 0:2, :, :].rearrange("p a j f -> p a (j f)")
        drop = o2[:, 2, :, :].rearrange("p j f -> p (j f)")
        den, acc = sumT[:, 0:2, :], sumT[:, 2:4, :]
        attn, attnT = x1[:, 0, :, :], x1[:, 1, :, :].rearrange("p j f -> p (j f)")
        rise, decay = (x1[:, n, :, :].rearrange("p j f -> p (j f)") for n in (2, 3))
        mx = sb("mx", [P, 4, GROUP + 1])
        rden = sb("rden", [P, TILES, HEADS])
        z3, o3 = xn, an
        xd = sb("xd", [P, 2, GROUP])
        same_row = xd[0:1, :, :].rearrange("p a e -> p (a e)").bitcast(BF16).rearrange("p (a e) -> p a e", e=GROUP)
        st3 = sb("st3", [P, TILES, 6])
        mv3 = sb("mv3", [P, 4, TILES, 2])
        sd3 = sb("sd3", [P, 4, TILES])
        rs3 = sb("rs3", [P, 4, TILES])
        nb3 = sb("nb3", [P, 4, TILES])

        banks = [ctx.enter_context(nc.psum_tensor(f"bank{i}", [P, GROUP], F32)) for i in range(8)]

        names = """weights_in ident_in bias_row_in zero_first rows_in tiles_in attr_tail_in zeroed bias_out bias_in masks_out rcount_out rcount_in
            consts_set zeros_set iota_done gate_sp gate_dve setup_v setup_t setup_c gate
            a_T a_same a_scan a_back a_mean a_mean_act
            w1_split n_T n_x_hi n_evac n_lo n_h n_relu n_y n_z n_stats n_aggr n_sd n_rs n_nb n_x1 n_x1_act n_z2 n_stats2 n_aggr2 n_sd2 n_rs2 n_nb2 n_out needs_made
            e_xd e_T e_evac e_q e_k e_v e_qT e_vT e_qk e_s e_mx e_keep e_drop e_rise e_decay e_prob e_pv e_den e_acc
            e_back e_rden e_attn e_attnT e_attnTs e_o e_z e_stats e_aggr e_sd e_rs e_nb e_out e_carry scattered stored needs_in""".split()
        s = {n: sem(n) for n in names}
        attr_in = [sem(f"attr_in{k}") for k in range(4)]
        zero_out = [sem(f"zero_out{k}") for k in range(ZFILLS)]
        dst_in = [sem(f"dst_in{k}") for k in range(4)]
        same_in = [sem(f"same_in{k}") for k in range(4)]
        mean_out = [sem(f"mean_out{k}") for k in range(4)]
        node_in = [sem(f"node_in{k}") for k in range(4)]
        x1_out = [sem(f"x1_out{k}") for k in range(4)]
        o2_out = [sem(f"o2_out{k}") for k in range(4)]
        reset_in = [sem(f"reset_in{k}") for k in range(4)]
        src_idx_in = [sem(f"src_idx_in{k}") for k in range(4)]
        out_idx_in = [sem(f"out_idx_in{k}") for k in range(4)]
        gathered = [sem(f"gathered{k}") for k in range(4)]
        o3_out = [sem(f"o3_out{k}") for k in range(4)]

        def steps(eng, total, lag, body, begin=0):
            first = -(-(4 + lag) // UNROLL) * UNROLL
            last = (total - 1) // UNROLL * UNROLL
            for g in range(begin, first):
                body(g, g % 4, g // 4)
            with eng.Fori(first // UNROLL, last // UNROLL) as i:
                for n in range(UNROLL):
                    body(i * UNROLL + n, n % 4, i * (UNROLL // 4) + n // 4)
            for g in range(last, total + lag):
                body(g, g % 4, g // 4)

        def inside(g, total):
            return not isinstance(g, int) or 0 <= g < total

        def wait(eng, semaphore, value):
            if not isinstance(value, int) or value > 0:
                eng.wait_ge(semaphore, value)

        def slot_count(g, k, per, back=0):
            if isinstance(g, int):
                return ((g - k) // 4 + 1 - back) * per
            return (g - k) * (per // 4) + (1 - back) * per

        def node_base(g):
            return min(g * GROUP, NODES - GROUP) if isinstance(g, int) else g * GROUP

        def node_rows(t, g):
            return t[bass.ds(node_base(g), GROUP), :].rearrange("(p j) f -> p j f", j=TILES)

        def node_zeros(g, k):
            per = ZSTEP // GROUP
            assert ZSTEP % GROUP == 0 and 4 % per == 0
            return g // per + 1 if isinstance(g, int) else (g - k) // per + k // per + 1

        def stand(eng, gate):
            eng.sem_inc(s[gate], 1)

        def all_uses(semaphores, total, per):
            return [(semaphores[k], slot_count((total - 1 - k) // 4 * 4 + k, k, per)) for k in range(4)]

        block = ctx.enter_context(nc.Block())

        @block.sync
        def _(sp):
            for t, src in ((cur_r, dst_row), (prev_r, prev_row)):
                sp.dma_start(t, src).then_inc(s["rows_in"], 16)
            sp.dma_start(ident[:, :], ident_c).then_inc(s["ident_in"], 16)

            def attr_load(g, k):
                wait(sp, s["a_T"], g - 3)
                stand(sp, "gate_sp")
                sp.dma_start(attr_sb[:, k, :, :],
                             attr[bass.ds(g * GROUP, GROUP), :].rearrange("(j p) f -> p j f", p=P))\
                    .then_inc(attr_in[k], 16)

            for g in range(4):
                attr_load(g, g)
            sp.wait_ge(s["setup_v"], 5)
            sp.dma_start(same_d.rearrange("(p c) -> p c", p=P), same_bf[:, :]).then_inc(s["masks_out"], 16)
            sp.dma_start(reset_d.rearrange("(p c) -> p c", p=P), reset_bf[:, :]).then_inc(s["masks_out"], 16)
            sp.wait_ge(s["setup_v"], 14)
            sp.dma_start(rcount_d.rearrange("(p c) -> p c", p=P), rcount_r).then_inc(s["rcount_out"], 16)
            sp.wait_ge(s["masks_out"], 32)

            def mask_load(g, k):
                wait(sp, s["a_T"], g - 3)
                stand(sp, "gate_sp")
                sp.dma_start(same_row[:, k, :], same_d[bass.ds(g * GROUP, GROUP)].unsqueeze(0))\
                    .then_inc(same_in[k], 16)

            for g in range(4):
                mask_load(g, g)
            sp.wait_ge(s["rcount_out"], 16)
            sp.dma_start(rcount_l, rcount_d.rearrange("(b t p) -> t b p", b=2, p=P))\
                .then_inc(s["rcount_in"], 16)
            sp.wait_ge(s["zeros_set"], 2)
            full = (EDGES - (EG - 1) * GROUP) // P
            rest = EDGES - (EG - 1) * GROUP - full * P
            tail = attr[(EG - 1) * GROUP:, :]
            sp.dma_start(attr_tail[:, 0:full, :], tail[0:full * P, :].rearrange("(j p) f -> p j f", p=P))\
                .then_inc(s["attr_tail_in"], 16)
            sp.dma_start(attr_tail[0:rest, full, :], tail[full * P:full * P + rest, :])\
                .then_inc(s["attr_tail_in"], 16)
            sp.wait_ge(s["setup_c"], 5)
            sp.dma_start(bias_d.rearrange("(a k) f -> a k f", a=1),
                         bias_part[:, :, :, :].rearrange("a k b f -> a (k b) f")).then_inc(s["bias_out"], 16)

            for t, src in (
                (w1_sb, w1.rearrange("(c p) h -> p c h", p=P)),
                (w2_sb[:, :, :], w2.rearrange("(c p) h -> p c h", p=P)),
                (head_sum[:, :], head_sum_c), (qkvw_sb[:, :], qkv_wT), (outw_sb[:, :], out_wT),
                (b1_sb[:, :], b1), (qkvb_sb[:, :], qkv_b), (outb_bc[:, :], out_b.to_broadcast((P, P))),
            ):
                sp.dma_start(t, src).then_inc(s["weights_in"], 16)

            def edge_load(g, k, _=None):
                if not isinstance(g, int) or 4 <= g < EG - 1:
                    attr_load(g, k)
                if not isinstance(g, int) or 4 <= g < EG:
                    mask_load(g, k)

            steps(sp, EG, 0, edge_load)
            sp.wait_ge(s["bias_out"], 16)
            sp.dma_start(bias3[:, :, :], bias_d.rearrange("(k b) f -> k b f", b=2)).then_inc(s["bias_in"], 16)

            sp.wait_ge(s["tiles_in"], 48)
            sp.wait_ge(s["setup_v"], 20)

            def layer1_loads(g, k, _=None):
                if inside(g, EG):
                    wait(sp, gathered[k], slot_count(g, k, 64, 1))
                    stand(sp, "gate_sp")
                    sp.dma_start(src_idx[:, k, :], src_i[:, bass.ds(g * TILES, TILES)]).then_inc(src_idx_in[k], 16)
                    wait(sp, s["e_keep"], g - 3)
                    stand(sp, "gate_sp")
                    sp.dma_start(reset_sb[:, k, :],
                                 reset_d[bass.ds(g * GROUP, GROUP)].unsqueeze(0).to_broadcast((P, GROUP)))\
                        .then_inc(reset_in[k], 16)
                h, m = g - 8, k
                if inside(h, EG):
                    wait(sp, o3_out[m], slot_count(h, m, 64, 1))
                    stand(sp, "gate_sp")
                    sp.dma_start(out_idx[:, m, :], scatter_i[:, bass.ds(h * TILES, TILES)])\
                        .then_inc(out_idx_in[m], 16)

            for g in range(4):
                layer1_loads(g, g)

            sp.wait_ge(s["needs_made"], 1)

            def mean_load(g, k):
                need = sp.value_load(need_scattered[:, bass.ds(g, 1)], min_val=1, max_val=EG)
                wait(sp, s["n_T"], g - 3)
                stand(sp, "gate_sp")
                sp.wait_ge(s["scattered"], need)
                stand(sp, "gate_sp")
                sp.wait_ge(s["zeroed"], node_zeros(g, k))
                if isinstance(g, int) and g == 3:
                    sp.wait_ge(s["a_scan"], EG)
                stand(sp, "gate_sp")
                sp.dma_start(an[:, k, :, :], node_rows(table_d, g)).then_inc(node_in[k], 16)

            mean_load(0, 0)

            def node_io(g, k, _=None):
                if inside(g, NG):
                    wait(sp, s["n_T"], g - 3)
                    wait(sp, s["n_z"], g - 3)
                    stand(sp, "gate_sp")
                    sp.dma_start(xn[:, k, :, :], node_rows(x, g)).then_inc(node_in[k], 16)
                if not isinstance(g, int) or g + 1 < NG:
                    mean_load(g + 1, (k + 1) % 4)
                h, m = g - 6, (k - 6) % 4
                if inside(h, NG):
                    sp.wait_ge(s["n_x1"], h + 1)
                    sp.wait_ge(s["n_x1_act"], h + 1)
                    if isinstance(h, int) and h == NG - 2:
                        sp.wait_ge(s["n_T"], NG)
                    if isinstance(h, int) and h == NG - 1:
                        sp.wait_ge(x1_out[(m - 1) % 4], slot_count(h - 1, (m - 1) % 4, 16))
                    stand(sp, "gate_sp")
                    sp.dma_start(node_rows(table_d, h), x1[:, m, :, :]).then_inc(x1_out[m], 16)
                h, m = g - 8, k
                if inside(h, NG):
                    sp.wait_ge(x1_out[m], slot_count(h, m, 16))
                    sp.sem_inc(s["stored"], 1)
                h, m = g - 9, (k - 9) % 4
                if inside(h, NG):
                    sp.wait_ge(s["n_out"], h + 1)
                    if isinstance(h, int) and h == NG - 1:
                        sp.wait_ge(o2_out[(m - 1) % 4], slot_count(h - 1, (m - 1) % 4, 16))
                    stand(sp, "gate_sp")
                    sp.dma_start(node_rows(out, h), o2[:, m, :, :]).then_inc(o2_out[m], 16)

            steps(sp, NG, 9, node_io)
            steps(sp, EG, 8, layer1_loads, begin=4)

        @block.gpsimd
        def _(pool):
            nc.gpsimd.iota(edge_no_i, pattern=[[1, EROW]], base=0, channel_multiplier=EROW)\
                .then_inc(s["iota_done"], 1)
            nc.gpsimd.iota(edge_end_i, pattern=[[0, 1]], base=GROUP, channel_multiplier=GROUP)\
                .then_inc(s["iota_done"], 1)
            nc.gpsimd.iota(base_i, pattern=[[GROUP, NG]], base=0, channel_multiplier=0).then_inc(s["iota_done"], 1)
            nc.gpsimd.iota(zbase_i, pattern=[[ZSTEP, EG]], base=0, channel_multiplier=0).then_inc(s["iota_done"], 1)

            def scatter(target, index, source, done):
                for j in range(TILES):
                    pool.indirect_dma_start(
                        out=target, out_offset=bass.IndirectOffsetOnAxis(ap=index[:, j:j + 1], axis=0),
                        in_=source(j), in_offset=None, bounds_check=NODES - 1, oob_is_err=False,
                    ).then_inc(done, 16)

            def gather(source, index, target, done):
                for j in range(TILES):
                    pool.indirect_dma_start(
                        out=target(j), out_offset=None, in_=source,
                        in_offset=bass.IndirectOffsetOnAxis(ap=index[:, j:j + 1], axis=0),
                        bounds_check=NODES - 1, oob_is_err=False,
                    ).then_inc(done, 16)

            pool.wait_ge(s["setup_v"], 20)
            pool.wait_ge(s["needs_made"], 1)

            for g in range(EG + 2):
                k, m = g % 4, (g - 2) % 4
                if g < EG:
                    pool.wait_ge(s["a_mean"], g + 1)
                    pool.wait_ge(s["a_mean_act"], g + 1)
                    pool.wait_ge(s["zeroed"], pool.value_load(need_zeroed[:, g:g + 1], min_val=1, max_val=EG))
                    stand(pool, "gate")
                    scatter(table_d, scatter_i[:, g * TILES:(g + 1) * TILES], lambda j: rows[:, g, j, :], mean_out[k])
                if g >= 2:
                    pool.wait_ge(mean_out[m], slot_count(g - 2, m, 64))
                    pool.sem_inc(s["scattered"], 1)

            def gather_dst(g):
                pool.wait_ge(s["stored"], pool.value_load(need_stored[:, g:g + 1], min_val=1, max_val=NG))
                wait(pool, dst_in[g % 4], slot_count(g, g % 4, 64, 1))
                stand(pool, "gate")
                gather(table_d, gather_i[:, g * TILES:(g + 1) * TILES], lambda j: rows[:, g, j, :], dst_in[g % 4])

            for g in range(EG - LATE):
                gather_dst(g)

            for semaphore, count in all_uses(x1_out, NG, 16):
                pool.wait_ge(semaphore, count)
            stand(pool, "gate")

            def layer1_rows(g, k, _=None):
                if inside(g, EG):
                    wait(pool, s["e_T"], g - 3)
                    pool.wait_ge(src_idx_in[k], slot_count(g, k, 16))
                    stand(pool, "gate")
                    gather(table_d, src_idx[:, k, :], lambda j: xs[:, k, j, :], gathered[k])
                if isinstance(g, int) and g < LATE:
                    gather_dst(EG - LATE + g)
                h, m = g - 10, (k - 10) % 4
                if inside(h, EG):
                    if isinstance(h, int) and h == 0:
                        for semaphore, count in all_uses(o2_out, NG, 16):
                            pool.wait_ge(semaphore, count)
                    pool.wait_ge(out_idx_in[m], slot_count(h, m, 16))
                    pool.wait_ge(s["e_out"], h + 1)
                    stand(pool, "gate")
                    scatter(out, out_idx[:, m, :], lambda j: o3[:, m, j, :], o3_out[m])

            steps(pool, EG, 10, layer1_rows)
            for semaphore, count in all_uses(o3_out, EG, 64):
                pool.wait_ge(semaphore, count)

        @block.scalar
        def _(act):
            for t, src in ((dst_i, dst_tile), (next_i, next_tile), (src_i[:, :], src_tile)):
                act.dma_start(t, src).then_inc(s["tiles_in"], 16)
            act.dma_start(first_i, first_dst.to_broadcast((NG, EG))).then_inc(s["needs_in"], 16)
            act.dma_start(last_i, last_dst).then_inc(s["needs_in"], 16)
            act.dma_start(bias_row[:, 0, :], b2).then_inc(s["bias_row_in"], 16)
            act.dma_start(bias_row[:, 1, :], out_b).then_inc(s["bias_row_in"], 16)
            act.wait_ge(s["zeros_set"], 1)
            act.wait_ge(s["rows_in"], 32)

            def zero_fill(z, done):
                base = min(z * ZSTEP, NODES - ZSTEP) if isinstance(z, int) else z * ZSTEP
                act.dma_start(table_d[bass.ds(base, ZSTEP), :].rearrange("(p a b) f -> p a (b f)", p=P, b=4),
                              zeros[:, :].unsqueeze(1).to_broadcast((P, ZROWS // 4, 4 * P))).then_inc(done, 16)

            for z in range(3):
                zero_fill(z, s["zero_first"])
            act.wait_ge(s["rcount_in"], 16)
            for z in (*range(3, ZFIRST), EG - 1):
                zero_fill(z, s["zero_first"])
            act.wait_ge(s["setup_c"], 7)

            def mean_act(g, k, q):
                if isinstance(g, int) and g == 3:
                    act.wait_ge(s["zero_first"], 16 * (ZFIRST + 1))
                    act.sem_inc(s["zeroed"], ZFIRST)
                if 1 <= k <= ZFILLS and (not isinstance(g, int) or g < EG):
                    if not isinstance(g, int) or g >= 4:
                        act.wait_ge(zero_out[k - 1], slot_count(g, k, 16, 1))
                        act.sem_inc(s["zeroed"], 1)
                    zero_fill(q * ZFILLS + k - 1 + ZFIRST, zero_out[k - 1])
                if inside(g, EG):
                    act.wait_ge(s["a_T"], g + 1)
                    wait(act, s["a_scan"], g - 1)
                    nc.scalar.activation(same_sb[:, k % 2, :], banks[4 + k % 2][:, :], ACT.Copy)\
                        .then_inc(s["a_same"], 1)
                h, m = g - 1, (k - 1) % 4
                if inside(h, EG):
                    act.wait_ge(s["a_back"], h + 1)
                    for j in range(TILES // 2, TILES):
                        i = nc.scalar.activation(rows[:, bass.ds(h, 1), j, :].rearrange("p g f -> p (g f)"),
                                                 banks[6 + m % 2][:, j * P:(j + 1) * P], ACT.Copy,
                                                 scale=rcount_t[:, bass.ds(h * TILES + j, 1)])
                    i.then_inc(s["a_mean_act"], 1)

            steps(act, EG, 1, mean_act)
            for done in zero_out:
                act.wait_ge(done, EG // 4 * 16)
                act.sem_inc(s["zeroed"], 1)
            act.sem_inc(s["zeroed"], 1)

            def node_act(g, k, _=None):
                if inside(g, NG):
                    act.wait_ge(s["n_T"], g + 1)
                    wait(act, s["n_h"], g - 1)
                    nc.scalar.activation(x_hi[:, k % 2, :], banks[0][:, :], ACT.Copy).then_inc(s["n_x_hi"], 1)
                    nc.scalar.activation(a_hi[:, k % 2, :], banks[1][:, :], ACT.Copy).then_inc(s["n_evac"], 1)
                h, m = g - 4, k
                if inside(h, NG):
                    act.wait_ge(s["n_aggr"], h + 1)
                    nc.scalar.activation(sd1[:, m, :], mv1[:, m, :, 1], ACT.Sqrt, bias=eps[:, :])\
                        .then_inc(s["n_sd"], 1)
                h, m = g - 6, (k - 6) % 4
                if inside(h, NG):
                    act.wait_ge(s["n_aggr2"], h + 1)
                    nc.scalar.activation(sd2[:, m, :], mv2[:, m, :, 1], ACT.Sqrt, bias=eps[:, :])\
                        .then_inc(s["n_sd2"], 1)
                h, m = g - 7, (k - 7) % 4
                if inside(h, NG):
                    act.wait_ge(s["n_nb2"], h + 1)
                    for j in range(TILES):
                        i = nc.scalar.activation(o2[:, m, j, :], o2[:, m, j, :], ACT.Identity,
                                                 bias=nb2[:, m, j:j + 1], scale=rs2[:, m, j:j + 1])
                    i.then_inc(s["n_out"], 1)
                h, m = g - 4, k
                if inside(h, NG):
                    act.wait_ge(s["n_nb"], h + 1)
                    for j in range(NORM1_DVE, TILES):
                        i = nc.scalar.activation(x1[:, m, j, :], x1[:, m, j, :], ACT.Identity,
                                                 bias=nb1[:, m, j:j + 1], scale=rs1[:, m, j:j + 1])
                    i.then_inc(s["n_x1_act"], 1)
                h, m = g - 1, (k - 1) % 4
                if inside(h, NG):
                    act.wait_ge(s["n_h"], h + 1)
                    wait(act, s["n_y"], h - 1)
                    for c in range(2):
                        i = nc.scalar.activation(hT[:, m % 2, c, :], banks[2 + 2 * (m % 2) + c][:, :], ACT.Relu,
                                                 bias=b1_sb[:, c:c + 1])
                    i.then_inc(s["n_relu"], 1)

            steps(act, NG, 7, node_act)

            act.wait_ge(s["n_x1"], NG)
            act.wait_ge(s["n_h"], NG)
            act.wait_ge(s["n_y"], NG)
            for semaphore, count in all_uses(o2_out, NG, 16):
                act.wait_ge(semaphore, count)

            def row_copy(h, m):
                if inside(h, EG):
                    act.wait_ge(dst_in[m], slot_count(h, m, 64))
                    wait(act, s["e_T"], h - 1)
                    nc.scalar.activation(xd[:, m % 2, :],
                                         rows[:, bass.ds(h, 1), :, :].rearrange("p g j f -> p (g j f)"), ACT.Copy)\
                        .then_inc(s["e_xd"], 1)

            row_copy(0, 0)

            def norm3(h, m, count):
                act.wait_ge(s["e_nb"], count)
                wait(act, o3_out[m], slot_count(h, m, 64, 1))
                for j in range(TILES):
                    i = nc.scalar.activation(o3[:, m, j, :], z3[:, m, j, :], ACT.Identity,
                                             bias=nb3[:, m, j:j + 1], scale=rs3[:, m, j:j + 1])
                i.then_inc(s["e_out"], 1)

            def edge_act(g, k, q):
                if inside(g, EG):
                    act.wait_ge(s["e_T"], g + 1)
                    wait(act, s["e_v"], g - 1)
                    nc.scalar.activation(xsT[:, k % 2, :], banks[0][:, :], ACT.Copy)
                    nc.scalar.activation(xdT[:, k % 2, :], banks[1][:, :], ACT.Copy).then_inc(s["e_evac"], 1)
                h, m = g - 1, (k - 1) % 4
                if inside(h, EG):
                    act.wait_ge(s["e_q"], h + 1)
                    wait(act, s["e_qk"], h)
                    nc.scalar.activation(qT, banks[2][:, :], ACT.Identity, bias=qkvb_sb[:, 0:1])\
                        .then_inc(s["e_qT"], 1)
                h = g - 8
                if k == 0 and inside(h, SINGLE):
                    act.wait_ge(s["e_aggr"], h + 4)
                    act.activation(sd3[:, :, :], mv3[:, :, :, 1], ACT.Sqrt, bias=eps[:, :]).then_inc(s["e_sd"], 1)
                h = g - 5
                if isinstance(h, int) and SINGLE <= h < EG:
                    act.wait_ge(s["e_aggr"], h + 1)
                    act.activation(sd3[:, h % 4, :], mv3[:, h % 4, :, 1], ACT.Sqrt, bias=eps[:, :])\
                        .then_inc(s["e_sd"], 1)
                h = g - 8
                if k > 0 and inside(h, SINGLE - 2):
                    norm3(h, k, q - 1)
                h, m = g - 1, (k - 1) % 4
                if inside(h, EG):
                    act.wait_ge(s["e_v"], h + 1)
                    wait(act, s["e_pv"], h - 1)
                    nc.scalar.activation(vT[:, m % 2, :], banks[2][:, :], ACT.Identity, bias=qkvb_sb[:, 2:3])\
                        .then_inc(s["e_vT"], 1)
                h = g - 4
                if inside(h, EG):
                    act.wait_ge(s["e_attnT"], h + 1)
                    wait(act, s["e_o"], h)
                    nc.scalar.activation(attnT, banks[6][:, :], ACT.Copy).then_inc(s["e_attnTs"], 1)
                h = g - 8
                if k == 0 and inside(h, SINGLE - 2):
                    norm3(h, k, q - 1)
                h = g - 2
                if inside(h, EG):
                    act.wait_ge(s["e_drop"], h + 1)
                    wait(act, s["e_acc"], h)
                    nc.scalar.activation(decay, drop, ACT.Exp).then_inc(s["e_decay"], 1)
                    act.wait_ge(s["e_rise"], h + 1)
                    nc.scalar.activation(prob[:, :], rise, ACT.Exp).then_inc(s["e_prob"], 1)

                row_copy(g + 1, (k + 1) % 4)
                if isinstance(g, int) and g == SINGLE + 5:
                    norm3(SINGLE - 2, 2, SINGLE // 4)
                    norm3(SINGLE - 1, 3, SINGLE // 4)
                h = g - 5
                if isinstance(h, int) and SINGLE <= h < EG:
                    norm3(h, h % 4, SINGLE // 4 + h - SINGLE + 1)

            steps(act, EG, 8, edge_act)

        @block.vector
        def _(dve):
            V = nc.vector
            done = [0, 0]

            def then(ins):
                done[0] += 1
                ins.then_inc(s["setup_v"], 1)
                dve.wait_ge(s["setup_v"], done[0])

            def thenc(ins):
                done[1] += 1
                ins.then_inc(s["setup_c"], 1)
                dve.wait_ge(s["setup_c"], done[1])

            V.memset(zeros[:, :], 0.0).then_inc(s["zeros_set"], 1)
            V.memset(attr_tail[:, :, :], 0.0).then_inc(s["zeros_set"], 1)
            V.memset(ones3[:, :], 1.0)
            V.memset(one1[:, :], 1.0)
            V.memset(start_row[:, :], 0.0)
            V.memset(mx[:, 0, 0:1], -FAR)
            V.memset(eps[:, :], EPS).then_inc(s["consts_set"], 1)
            dve.wait_ge(s["rows_in"], 32)
            dve.wait_ge(s["iota_done"], 4)
            dve.wait_ge(s["consts_set"], 1)
            then(V.tensor_copy(cur_rf, cur_r))
            then(V.tensor_copy(prev_rf, prev_r))
            then(V.tensor_tensor(same_r, cur_rf, prev_rf, ALU.is_equal))
            then(V.tensor_copy(same_bf[:, :], same_r))
            then(V.tensor_scalar(reset_bf[:, :], same_r, 2.0 * FAR, -FAR, ALU.mult, ALU.add))
            then(V.tensor_copy(edge_no, edge_no_i))
            then(V.tensor_tensor(first_r, edge_no, same_r, ALU.mult))
            then(V.tensor_tensor(first_r, edge_no, first_r, ALU.subtract))
            then(V.tensor_tensor_scan(start_r, first_r, first_r, 0.0, ALU.max, ALU.max))
            dve.wait_ge(s["setup_t"], 1)
            then(V.tensor_tensor_scan(start_row[:, 1:P + 1], banks[7][0:1, 0:P], start_row[:, 0:1].to_broadcast((1, P)),
                                      0.0, ALU.max, ALU.max))
            dve.wait_ge(s["setup_t"], 2)
            then(V.tensor_copy(start_in[:, :], banks[6][:, 0:1]))
            then(V.tensor_scalar(count_r, start_r, start_in[:, :], None, ALU.max))
            then(V.scalar_tensor_tensor(count_r, edge_no, 1.0, count_r, ALU.add, ALU.subtract))
            then(V.reciprocal(rcount_r, count_r))
            dve.wait_ge(s["tiles_in"], 48)
            then(V.tensor_copy(dst_f, dst_i))
            then(V.tensor_copy(next_f, next_i))
            then(V.tensor_tensor(inner_f, dst_f, next_f, ALU.is_equal))
            then(V.scalar_tensor_tensor(scatter_f, inner_f, SKIP, dst_f, ALU.mult, ALU.add))
            then(V.tensor_copy(scatter_i[:, :], scatter_f))
            then(V.tensor_scalar(gather_i[:, :], dst_f, float(NODES - 1), None, ALU.min))
            dve.wait_ge(s["needs_in"], 32)
            then(V.memset(needs[:, :], 1.0))
            then(V.tensor_copy(first_f, first_i))
            then(V.tensor_copy(edge_end, edge_end_i))
            then(V.tensor_scalar(last_f, last_i, float(NODES - 1), None, ALU.min))
            then(V.tensor_scalar(base_f, base_i, float(NODES - GROUP), None, ALU.min))
            then(V.tensor_scalar(zbase_f, zbase_i, float(NODES - ZSTEP), None, ALU.min))
            then(V.tensor_scalar(first_c, first_f, edge_end[0:NG, :], None, ALU.is_lt, ALU.add,
                                 accum_out=needs[0:NG, 0:1]))
            then(V.tensor_scalar(base_c, base_f, last_f, None, ALU.is_le, ALU.add, accum_out=needs[0:EG, 1:2]))
            then(V.tensor_scalar(zbase_c, zbase_f, last_f, None, ALU.is_le, ALU.add, accum_out=needs[0:EG, 2:3]))
            dve.wait_ge(s["setup_t"], 3)
            V.tensor_scalar(needs_i[:, :], banks[7][0:1, 0:3 * P], 1.0, None, ALU.max).then_inc(s["needs_made"], 1)
            dve.wait_ge(s["bias_row_in"], 32)
            thenc(V.tensor_copy(bias_part[:, 0, :, :], bias_row[:, :, :]))
            thenc(V.tensor_tensor(bias_left[:, 0, :, :], bias_row[:, :, :], bias_part[:, 0, :, :], ALU.subtract))
            thenc(V.tensor_copy(bias_part[:, 1, :, :], bias_left[:, 0, :, :]))
            thenc(V.tensor_tensor(bias_left[:, 1, :, :], bias_left[:, 0, :, :], bias_part[:, 1, :, :], ALU.subtract))
            thenc(V.tensor_copy(bias_part[:, 2, :, :], bias_left[:, 1, :, :]))
            dve.wait_ge(s["setup_t"], 5)
            for b in range(2):
                V.tensor_copy(rcount_t[:, b * (ET // 2):(b + 1) * (ET // 2)], banks[6][:, b * P:b * P + ET // 2])\
                    .then_inc(s["setup_c"], 1)

            def sums(g, k, _=None):
                if inside(g, EG):
                    dve.wait_ge(s["a_same"], g + 1)
                    wait(dve, s["a_back"], g - 3)
                    wait(dve, s["a_scan"], g)
                    start = 0.0 if isinstance(g, int) and g == 0 else sumT[:, (k - 1) % 4, GROUP - 1:GROUP]
                    V.tensor_tensor_scan(sumT[:, k, :], same_sb[:, k % 2, :], banks[k % 2][:, :], start,
                                         ALU.mult, ALU.add).then_inc(s["a_scan"], 1)
                h, m = g - 1, (k - 1) % 4
                if inside(h, EG):
                    dve.wait_ge(s["a_back"], h + 1)
                    for j in range(TILES // 2):
                        i = V.tensor_scalar(rows[:, bass.ds(h, 1), j, :].rearrange("p g f -> p (g f)"),
                                            banks[2 + m % 2][:, j * P:(j + 1) * P],
                                            rcount_t[:, bass.ds(h * TILES + j, 1)], None, ALU.mult)
                    i.then_inc(s["a_mean"], 1)

            steps(dve, EG, 1, sums)

            dve.wait_ge(s["weights_in"], 16 * 8)
            V.tensor_copy(w1_hi[:, :, :], w1_sb).then_inc(s["w1_split"], 1)
            dve.wait_ge(s["w1_split"], 1)
            V.tensor_tensor(w1_lo[:, :, :], w1_sb, w1_hi[:, :, :], ALU.subtract).then_inc(s["w1_split"], 1)

            def node_dve(g, k, _=None):
                z, n, r, t = g - 3, g - 4, g - 5, g - 6
                kz, kr, kt = (k - 3) % 4, (k - 5) % 4, (k - 6) % 4
                if inside(z, NG):
                    dve.wait_ge(s["n_y"], z + 1)
                    wait(dve, x1_out[kz], slot_count(z, kz, 16, 1))
                    V.tensor_tensor(x1[:, kz, :, :].rearrange("p j f -> p (j f)"), banks[6 + kz % 2][:, :],
                                    xn[:, kz, :, :].rearrange("p j f -> p (j f)"), ALU.add).then_inc(s["n_z"], 1)
                if inside(n, NG):
                    dve.wait_ge(s["n_sd"], n + 1)
                    V.reciprocal(rs1[:, k, :], sd1[:, k, :]).then_inc(s["n_rs"], 1)
                if inside(g, NG):
                    dve.wait_ge(s["n_x_hi"], g + 1)
                    wait(dve, s["n_h"], g - 1)
                    V.tensor_tensor(x_lo[:, k % 2, :], banks[0][:, :], x_hi[:, k % 2, :], ALU.subtract)
                if inside(n, NG):
                    dve.wait_ge(s["n_rs"], n + 1)
                    V.scalar_tensor_tensor(nb1[:, k, :], mv1[:, k, :, 0], -1.0, rs1[:, k, :], ALU.mult, ALU.mult)\
                        .then_inc(s["n_nb"], 1)
                if inside(g, NG):
                    dve.wait_ge(s["n_evac"], g + 1)
                    V.tensor_tensor(a_lo[:, k % 2, :], banks[1][:, :], a_hi[:, k % 2, :], ALU.subtract)\
                        .then_inc(s["n_lo"], 1)
                if inside(n, NG):
                    for j in range(NORM1_DVE):
                        i = V.tensor_scalar(x1[:, k, j, :], x1[:, k, j, :], mv1[:, k, j, 0:1], rs1[:, k, j:j + 1],
                                            ALU.subtract, ALU.mult)
                    i.then_inc(s["n_x1"], 1)
                if inside(z, NG):
                    dve.wait_ge(s["n_z"], z + 1)
                    stand(dve, "gate_dve")
                    for j in range(TILES):
                        i = V.bn_stats(st1[:, kz % 2, j, :], x1[:, kz, j, :])
                    i.then_inc(s["n_stats"], 1)
                if inside(r, NG):
                    dve.wait_ge(s["n_x1"], r + 1)
                    dve.wait_ge(s["n_x1_act"], r + 1)
                    wait(dve, o2_out[kr], slot_count(r, kr, 16, 1))
                    V.tensor_tensor(o2[:, kr, :, :], x1[:, kr, :, :],
                                    outb_bc[:, :].unsqueeze(1).to_broadcast((P, TILES, P)), ALU.add)\
                        .then_inc(s["n_z2"], 1)
                if inside(z, NG):
                    dve.wait_ge(s["n_stats"], z + 1)
                    stand(dve, "gate_dve")
                    for j in range(TILES):
                        i = V.bn_aggr(mv1[:, kz, j, :], st1[:, kz % 2, j, :])
                    i.then_inc(s["n_aggr"], 1)
                if inside(r, NG):
                    dve.wait_ge(s["n_z2"], r + 1)
                    stand(dve, "gate_dve")
                    for j in range(TILES):
                        i = V.bn_stats(st2[:, kr % 2, j, :], o2[:, kr, j, :])
                    i.then_inc(s["n_stats2"], 1)
                if inside(t, NG):
                    dve.wait_ge(s["n_sd2"], t + 1)
                    V.reciprocal(rs2[:, kt, :], sd2[:, kt, :]).then_inc(s["n_rs2"], 1)
                if inside(r, NG):
                    dve.wait_ge(s["n_stats2"], r + 1)
                    stand(dve, "gate_dve")
                    for j in range(TILES):
                        i = V.bn_aggr(mv2[:, kr, j, :], st2[:, kr % 2, j, :])
                    i.then_inc(s["n_aggr2"], 1)
                if inside(t, NG):
                    dve.wait_ge(s["n_rs2"], t + 1)
                    V.scalar_tensor_tensor(nb2[:, kt, :], mv2[:, kt, :, 0], -1.0, rs2[:, kt, :], ALU.mult, ALU.mult)\
                        .then_inc(s["n_nb2"], 1)

            steps(dve, NG, 6, node_dve)

            def edge_dve(g, k, q):
                d, n = g - 4, g - 2
                m = (k - 2) % 4
                has_d, has_n, has_q = inside(d, EG), inside(n, EG), inside(g - 1, EG)
                if has_d:
                    dve.wait_ge(s["e_back"], d + 1)
                    V.reciprocal(rden[:, :, :].rearrange("p j h -> p (j h)"), banks[4][:, 0:GROUP:HD])\
                        .then_inc(s["e_rden"], 1)
                if has_n:
                    dve.wait_ge(s["e_s"], n + 1)
                    dve.wait_ge(reset_in[m], slot_count(n, m, 16))
                    wait(dve, s["e_carry"], n)
                    V.tensor_tensor_scan(mx[:, m, 1:GROUP + 1], reset_sb[:, m, :], banks[5][:, :],
                                         mx[:, m, 0:1], ALU.min, ALU.max).then_inc(s["e_mx"], 1)
                if has_d:
                    dve.wait_ge(s["e_rden"], d + 1)
                    wait(dve, s["e_attnT"], d)
                    V.tensor_tensor(attn[:, :, :].rearrange("p j (h d) -> p (j h) d", d=HD),
                                    banks[6][:, :].rearrange("p (a d) -> p a d", d=HD),
                                    rden[:, :, :].rearrange("p j h -> p (j h)").unsqueeze(2)
                                    .to_broadcast((P, TILES * HEADS, HD)), ALU.mult).then_inc(s["e_attn"], 1)
                if has_n:
                    dve.wait_ge(s["e_mx"], n + 1)
                    V.tensor_tensor(keep, mx[:, m, 0:GROUP], reset_sb[:, m, :], ALU.min)\
                        .then_inc(s["e_keep"], 1)
                h = g - 8
                if k == 0 and inside(h, SINGLE):
                    dve.wait_ge(s["e_sd"], q - 1)
                    wait(dve, s["e_out"], h)
                    V.reciprocal(rs3[:, :, :], sd3[:, :, :]).then_inc(s["e_rs"], 1)
                    dve.wait_ge(s["e_rs"], q - 1)
                    V.scalar_tensor_tensor(nb3[:, :, :], mv3[:, :, :, 0], -1.0, rs3[:, :, :], ALU.mult, ALU.mult)\
                        .then_inc(s["e_nb"], 1)
                h = g - 5
                if isinstance(h, int) and SINGLE <= h < EG:
                    slot, count = h % 4, SINGLE // 4 + h - SINGLE + 1
                    dve.wait_ge(s["e_sd"], count)
                    dve.wait_ge(s["e_out"], h - 3)
                    V.reciprocal(rs3[:, slot, :], sd3[:, slot, :]).then_inc(s["e_rs"], 1)
                    dve.wait_ge(s["e_rs"], count)
                    V.scalar_tensor_tensor(nb3[:, slot, :], mv3[:, slot, :, 0], -1.0, rs3[:, slot, :], ALU.mult, ALU.mult)\
                        .then_inc(s["e_nb"], 1)
                if has_q:
                    h = g - 1
                    dve.wait_ge(s["e_qT"], h + 1)
                    dve.wait_ge(s["e_k"], h + 1)
                    wait(dve, s["e_s"], h - 1)
                    V.scalar_tensor_tensor(qk[:, (k - 1) % 2, :], banks[3][:, :], qkvb_sb[:, 1:2], qT,
                                           ALU.add, ALU.mult).then_inc(s["e_qk"], 1)
                if has_n:
                    V.tensor_copy(mx[:, (m + 1) % 4, 0:1], mx[:, m, GROUP:GROUP + 1]).then_inc(s["e_carry"], 1)
                    dve.wait_ge(s["e_keep"], n + 1)
                    wait(dve, s["e_decay"], n)
                    V.tensor_tensor(drop, keep, mx[:, m, 1:GROUP + 1], ALU.subtract)\
                        .then_inc(s["e_drop"], 1)
                    wait(dve, s["e_prob"], n)
                    V.tensor_tensor(rise, banks[5][:, :], mx[:, m, 1:GROUP + 1], ALU.subtract)\
                        .then_inc(s["e_rise"], 1)
                if has_d:
                    dve.wait_ge(s["e_o"], d + 1)
                    wait(dve, s["e_out"], d - 3)
                    V.tensor_tensor(z3[:, k, :, :].rearrange("p j f -> p (j f)"), banks[7][:, :],
                                    rows[:, bass.ds(d, 1), :, :].rearrange("p g j f -> p (g j f)"), ALU.add)\
                        .then_inc(s["e_z"], 1)

                def weigh():
                    if has_n:
                        dve.wait_ge(s["e_prob"], n + 1)
                        dve.wait_ge(s["e_vT"], n + 1)
                        V.tensor_tensor(pv[:, :], vT[:, m % 2, :], prob[:, :], ALU.mult).then_inc(s["e_pv"], 1)

                def stats():
                    if has_d:
                        dve.wait_ge(s["e_z"], d + 1)
                        stand(dve, "gate_dve")
                        for j in range(TILES):
                            i = V.bn_stats(st3[:, j, :], z3[:, k, j, :])
                        i.then_inc(s["e_stats"], 1)

                if k == 0:
                    stats()
                    weigh()
                else:
                    weigh()
                    stats()
                if has_n:
                    first = isinstance(n, int) and n == 0
                    dve.wait_ge(s["e_decay"], n + 1)
                    wait(dve, s["e_den"], n)
                    wait(dve, s["e_back"], n - 1)
                    V.tensor_tensor_scan(den[:, m % 2, :], decay, prob[:, :],
                                         0.0 if first else den[:, (m + 1) % 2, GROUP - 1:GROUP],
                                         ALU.mult, ALU.add).then_inc(s["e_den"], 1)
                    dve.wait_ge(s["e_pv"], n + 1)
                    wait(dve, s["e_acc"], n)
                    V.tensor_tensor_scan(acc[:, m % 2, :], decay, pv[:, :],
                                         0.0 if first else acc[:, (m + 1) % 2, GROUP - 1:GROUP],
                                         ALU.mult, ALU.add).then_inc(s["e_acc"], 1)
                if has_d:
                    dve.wait_ge(s["e_stats"], d + 1)
                    stand(dve, "gate_dve")
                    for j in range(TILES):
                        i = V.bn_aggr(mv3[:, k, j, :], st3[:, j, :])
                    i.then_inc(s["e_aggr"], 1)

            steps(dve, EG, 8, edge_dve)

        @block.tensor
        def _(pe):
            T = nc.tensor
            pe.wait_ge(s["ident_in"], 16)
            pe.wait_ge(s["consts_set"], 1)
            pe.wait_ge(s["setup_v"], 9)
            T.transpose(banks[7][0:1, 0:P], start_r[:, EROW - 1:EROW], ident[:, :]).then_inc(s["setup_t"], 1)
            pe.wait_ge(s["setup_v"], 10)
            T.matmul(banks[6][:, 0:1], start_row[:, 0:P], one1[:, :], start=True, stop=True)\
                .then_inc(s["setup_t"], 1)
            pe.wait_ge(s["setup_v"], 29)
            for c in range(3):
                i = T.transpose(banks[7][0:1, c * P:(c + 1) * P], needs[:, c:c + 1], ident[:, :])
            i.then_inc(s["setup_t"], 1)
            pe.wait_ge(s["rcount_in"], 16)
            for b in range(2):
                T.transpose(banks[6][:, b * P:b * P + ET // 2], rcount_l[:, b, :], ident[0:ET // 2, 0:ET // 2])\
                    .then_inc(s["setup_t"], 1)
            pe.wait_ge(s["attr_tail_in"], 32)

            def edge_sums(g, k, _=None):
                if inside(g, EG):
                    last = isinstance(g, int) and g == EG - 1
                    if not last:
                        pe.wait_ge(attr_in[k], slot_count(g, k, 16))
                    wait(pe, s["a_scan"], g - 1)
                    for j in range(TILES):
                        src = attr_tail[:, j, :] if last else attr_sb[:, k, j, :]
                        T.transpose(banks[k % 2][:, j * P:(j + 1) * P], src, ident[:, :])
                    pe.wait_ge(same_in[k], slot_count(g, k, 16))
                    T.matmul(banks[4 + k % 2][:, :], ones3[0:1, :], same_row[:, k, :], start=True, stop=True)\
                        .then_inc(s["a_T"], 1)
                h, m = g - 1, (k - 1) % 4
                if inside(h, EG):
                    pe.wait_ge(s["a_scan"], h + 1)
                    wait(pe, s["a_mean"], h - 1)
                    wait(pe, s["a_mean_act"], h - 1)
                    for j in range(TILES):
                        i = T.transpose(banks[2 + 4 * (j // 2) + m % 2][:, j * P:(j + 1) * P], sumT[:, m, j * P:(j + 1) * P],
                                        ident[:, :])
                    i.then_inc(s["a_back"], 1)

            steps(pe, EG, 1, edge_sums)
            pe.wait_ge(s["a_mean"], EG)
            pe.wait_ge(s["a_mean_act"], EG)
            pe.wait_ge(s["weights_in"], 16 * 8)
            pe.wait_ge(s["w1_split"], 2)
            pe.wait_ge(s["setup_c"], 7)
            pe.wait_ge(s["bias_in"], 16)

            def node_pe(g, k, _=None):
                if inside(g, NG):
                    pe.wait_ge(node_in[k], slot_count(g, k, 32))
                    wait(pe, s["n_evac"], g)
                    wait(pe, s["n_lo"], g)
                    for src, bank in ((xn, 0), (an, 1)):
                        for j in range(TILES):
                            i = T.transpose(banks[bank][:, j * P:(j + 1) * P], src[:, k, j, :], ident[:, :])
                    i.then_inc(s["n_T"], 1)
                h, m = g - 1, (k - 1) % 4
                if inside(h, NG):
                    pe.wait_ge(s["n_evac"], h + 1)
                    wait(pe, s["n_relu"], h - 1)
                    pe.wait_ge(s["n_lo"], h + 1)
                    for c in range(2):
                        bank, cols = banks[2 + 2 * (m % 2) + c], slice(c * P, (c + 1) * P)
                        parts = [(w1_hi[:, 0, cols], x_hi), (w1_hi[:, 1, cols], a_hi),
                                 (w1_lo[:, 0, cols], x_hi), (w1_lo[:, 1, cols], a_hi),
                                 (w1_hi[:, 0, cols], x_lo), (w1_hi[:, 1, cols], a_lo)]
                        for n, (left, right) in enumerate(parts):
                            i = T.matmul(bank[:, :], left, right[:, m % 2, :], start=(n == 0), stop=(n == 5))
                    i.then_inc(s["n_h"], 1)
                h, m = g - 2, (k - 2) % 4
                if inside(h, NG):
                    pe.wait_ge(s["n_relu"], h + 1)
                    wait(pe, s["n_z"], h - 1)
                    bank = banks[6 + m % 2]
                    T.matmul(bank[:, :], ones3[:, :], bias3[:, 0, :].unsqueeze(1).to_broadcast((3, TILES, P)),
                             start=True, stop=False)
                    for j in range(TILES):
                        for c in range(2):
                            i = T.matmul(bank[:, j * P:(j + 1) * P], hT[:, m % 2, c, j * P:(j + 1) * P],
                                         w2_sb[:, c, :], start=False, stop=(c == 1 and j == TILES - 1))
                    i.then_inc(s["n_y"], 1)

            steps(pe, NG, 2, node_pe)
            pe.wait_ge(s["n_z"], NG)
            pe.wait_ge(s["n_relu"], NG)

            def edge_pe(g, k, _=None):
                h, m = g - 2, (k - 2) % 4
                if inside(h, EG):
                    pe.wait_ge(s["e_qk"], h + 1)
                    wait(pe, s["e_rise"], h)
                    T.matmul(banks[5][:, :], head_sum[:, :], qk[:, m % 2, :], start=True, stop=True)\
                        .then_inc(s["e_s"], 1)
                if inside(g, EG):
                    pe.wait_ge(gathered[k], slot_count(g, k, 64))
                    wait(pe, s["e_evac"], g)
                    for j in range(TILES):
                        T.transpose(banks[0][:, j * P:(j + 1) * P], xs[:, k, j, :], ident[:, :])
                    pe.wait_ge(s["e_xd"], g + 1)
                    for j in range(TILES):
                        i = T.transpose(banks[1][:, j * P:(j + 1) * P], xd[:, k % 2, j * P:(j + 1) * P], ident[:, :])
                    i.then_inc(s["e_T"], 1)
                h, m = g - 1, (k - 1) % 4
                if inside(h, EG):
                    pe.wait_ge(s["e_evac"], h + 1)
                    wait(pe, s["e_vT"], h)
                    T.matmul(banks[2][:, :], qkvw_sb[:, 0:P], xdT[:, m % 2, :], start=True, stop=True)\
                        .then_inc(s["e_q"], 1)
                    wait(pe, s["e_qk"], h)
                    T.matmul(banks[3][:, :], qkvw_sb[:, P:2 * P], xsT[:, m % 2, :], start=True, stop=True)\
                        .then_inc(s["e_k"], 1)
                    pe.wait_ge(s["e_qT"], h + 1)
                    T.matmul(banks[2][:, :], qkvw_sb[:, 2 * P:3 * P], xsT[:, m % 2, :], start=True, stop=True)\
                        .then_inc(s["e_v"], 1)
                h, m = g - 4, k
                if inside(h, EG):
                    pe.wait_ge(s["e_attn"], h + 1)
                    for j in range(TILES):
                        i = T.transpose(banks[6][:, j * P:(j + 1) * P], attn[:, j, :], ident[:, :])
                    i.then_inc(s["e_attnT"], 1)
                h, m = g - 4, k
                if inside(h, EG):
                    pe.wait_ge(s["e_attnTs"], h + 1)
                    wait(pe, s["e_z"], h)
                    T.matmul(banks[7][:, :], ones3[:, :], bias3[:, 1, :].unsqueeze(1).to_broadcast((3, TILES, P)),
                             start=True, stop=False)
                    for j in range(TILES):
                        i = T.matmul(banks[7][:, j * P:(j + 1) * P], attnT[:, j * P:(j + 1) * P], outw_sb[:, :],
                                     start=False, stop=(j == TILES - 1))
                    i.then_inc(s["e_o"], 1)
                h, m = g - 3, (k - 3) % 4
                if inside(h, EG):
                    pe.wait_ge(s["e_acc"], h + 1)
                    wait(pe, s["e_attnTs"], h)
                    wait(pe, s["e_rden"], h)
                    for j in range(TILES):
                        T.transpose(banks[6][:, j * P:(j + 1) * P], acc[:, m % 2, j * P:(j + 1) * P], ident[:, :])
                    for j in range(TILES):
                        i = T.transpose(banks[4][:, j * P:(j + 1) * P], den[:, m % 2, j * P:(j + 1) * P], ident[:, :])
                    i.then_inc(s["e_back"], 1)

            steps(pe, EG, 4, edge_pe)


def kernel(x, src, dst, edge_attr_128, L0_gnn_W1, L0_gnn_b1, L0_gnn_W2, L0_gnn_b2, L1_gnn_qkv_w, L1_gnn_qkv_b,
           L1_gnn_out_w, L1_gnn_out_b):
    import numpy as np
    import concourse.bacc as bacc
    from concourse.bass_utils import run_bass_kernel_spmd as run

    src, dst = np.asarray(src), np.asarray(dst)
    pad = EPAD - EDGES
    dst_p = np.concatenate([dst, np.full(pad, PAD_NODE, dst.dtype)])
    next_p = np.concatenate([dst[1:], np.full(pad + 1, PAD_NODE, dst.dtype)])
    prev_p = np.concatenate([np.full(1, -1, dst.dtype), dst_p[:-1]])
    src_p = np.concatenate([src, np.zeros(pad, src.dtype)])
    head = np.arange(P) // HD
    ins = {
        "x": x, "attr": edge_attr_128,
        "dst_tile": dst_p.reshape(ET, P).T, "next_tile": next_p.reshape(ET, P).T, "src_tile": src_p.reshape(ET, P).T,
        "first_dst": dst_p[::GROUP].reshape(1, EG), "last_dst": dst_p[GROUP - 1::GROUP].reshape(EG, 1),
        "dst_row": dst_p.reshape(P, EROW), "prev_row": prev_p.reshape(P, EROW),
        "w1": L0_gnn_W1, "b1": np.asarray(L0_gnn_b1).reshape(2, P).T,
        "w2": L0_gnn_W2, "b2": np.asarray(L0_gnn_b2).reshape(1, P),
        "qkv_wT": np.asarray(L1_gnn_qkv_w).T, "qkv_b": np.asarray(L1_gnn_qkv_b).reshape(3, P).T,
        "out_wT": np.asarray(L1_gnn_out_w).T, "out_b": np.asarray(L1_gnn_out_b).reshape(1, P),
        "ident_c": np.eye(P, dtype=np.float32),
        "head_sum_c": (head[:, None] == head[None, :]).astype(np.float32) * np.float32(HD ** -0.5),
    }
    ins = {k: np.ascontiguousarray(v) for k, v in ins.items()}
    nc = bacc.Bacc("TRN2", target_bir_lowering=False, num_devices=1)
    args = {k: nc.dram_tensor(k, v.shape, mybir.dt.from_np(v.dtype), kind="ExternalInput").ap()
            for k, v in ins.items()}
    out = nc.dram_tensor("out", (NODES, P), F32, kind="ExternalOutput").ap()
    build(nc, out=out, **args)
    r = run(nc, [ins], core_ids=[0])
    return r.results[0]["out"]
```
